# Optimizing a Trainium2 kernel written in Bass

```python
import numpy as np
import jax
import jax.numpy as jnp

def _softmax(x, axis=-1):
    return jax.nn.softmax(x, axis=axis)

def _gelu(x):
    return jax.nn.gelu(x, approximate=True)

def _silu(x):
    return jax.nn.silu(x)

def _sigmoid(x):
    return jax.nn.sigmoid(x)

def _layernorm(x, axis=-1, eps=1e-05):
    m = jnp.mean(x, axis=axis, keepdims=True)
    v = jnp.var(x, axis=axis, keepdims=True)
    return (x - m) / jnp.sqrt(v + eps)

def _scatter_add(tgt, idx, src, axis=0):
    return tgt.at[idx].add(src)

def _segment_sum(src, seg, n):
    return jax.ops.segment_sum(src, seg, n)
kernel_name = 'mk_flamingo_gated_d2_seqx_r4_555cb6'

def setup_inputs(seed: int=0):
    np.random.seed(seed)
    _w = jnp.asarray

    def _rec_inputs():
        import jax
        import jax.numpy as jnp
        _rk = jax.random.key(seed)
        x = 7.22e-05 + 1 * jax.random.normal(jax.random.fold_in(_rk, 1), (1, 2048, 256), jnp.float32)
        _lenS = 2048 - jax.random.randint(jax.random.fold_in(_rk, 7), (1,), 0, max(1, 2048 // 4) + 1, jnp.int32)
        _lenS2 = 1601 - jax.random.randint(jax.random.fold_in(_rk, 8), (1,), 0, max(1, 1601 // 4) + 1, jnp.int32)
        _ctx_768P = jax.random.normal(jax.random.fold_in(_rk, 11), (1, 16, 192), jnp.float32)
        _ctx_768c = jax.random.dirichlet(jax.random.fold_in(_rk, 511), 0.3 * jnp.ones((16,), jnp.float32), (1, 1601))
        _ctx_768t = jnp.einsum('bsk,bkd->bsd', _ctx_768c, _ctx_768P)
        _ctx_768t = _ctx_768t * jax.lax.rsqrt(jnp.mean(jnp.square(_ctx_768t)) + 1e-12) * 0.953939
        ctx_768 = -0.000191848 + 0.999787 * (_ctx_768t + 0.3 * jax.random.normal(jax.random.fold_in(_rk, 611), (1, 1601, 192), jnp.float32))
        _g = jax.random.normal(jax.random.fold_in(_rk, 9001), (2, 2), jnp.float32)
        _g = jnp.sign(_g) * jnp.maximum(jnp.abs(_g), 1.0) + (_g == 0) * 1.0
        g_xattn = _g[0]
        g_ffn = _g[1]
        return (x, ctx_768, g_xattn, g_ffn)
    x, ctx_768, g_xattn, g_ffn = _rec_inputs()

    def _L0_xattn_setup():
        import jax, jax.numpy as jnp
        import numpy as np
        N_HEADS = 16
        key = jax.random.key(seed)
        ks = jax.random.split(key, 8)
        b, l, m = (8, 256, 256)
        d_embed, d_cross = (256, 192)
        s_q = 1.0 / np.sqrt(d_embed)
        s_kv = 1.0 / np.sqrt(d_cross)
        return {'x': jax.random.normal(ks[0], (b, l, d_embed), jnp.float32), 'y': jax.random.normal(ks[1], (b, m, d_cross), jnp.float32), 'Wq': jax.random.normal(ks[2], (d_embed, d_embed), jnp.float32) * s_q, 'bq': jax.random.normal(ks[3], (d_embed,), jnp.float32) * 0.01, 'Wkv': jax.random.normal(ks[4], (2 * d_embed, d_cross), jnp.float32) * s_kv, 'bkv': jax.random.normal(ks[5], (2 * d_embed,), jnp.float32) * 0.01, 'Wo': jax.random.normal(ks[6], (d_embed, d_embed), jnp.float32) * s_q, 'bo': jax.random.normal(ks[7], (d_embed,), jnp.float32) * 0.01}
    _L0_xattn_all = _L0_xattn_setup()
    _L0_xattn_in = {k: v for k, v in _L0_xattn_all.items() if k in ('Wq', 'bq', 'Wkv', 'bkv', 'Wo', 'bo')}
    del _L0_xattn_all

    def _L0_ffn_setup():
        import jax, jax.numpy as jnp
        import numpy as np
        B, S, H, F, E = (1, 512, 256, 512, 8)

        def _swiglu(x, wg, wu, wd):
            return jax.nn.silu(x @ wg.T) * (x @ wu.T) @ wd.T
        key = jax.random.key(seed)
        ks = jax.random.split(key, 8)
        sc = 1.0 / np.sqrt(H)
        scf = 1.0 / np.sqrt(F)
        return {'hidden_states': jax.random.normal(ks[0], (B, S, H), jnp.float32), 'gate_w': jax.random.normal(ks[1], (E, H), jnp.float32) * sc, 'shared_gate': jax.random.normal(ks[2], (F, H), jnp.float32) * sc, 'shared_up': jax.random.normal(ks[3], (F, H), jnp.float32) * sc, 'shared_down': jax.random.normal(ks[4], (H, F), jnp.float32) * scf, 'r_gate': jax.random.normal(ks[5], (E, F, H), jnp.float32) * sc, 'r_up': jax.random.normal(ks[6], (E, F, H), jnp.float32) * sc, 'r_down': jax.random.normal(ks[7], (E, H, F), jnp.float32) * scf}
    _L0_ffn_all = _L0_ffn_setup()
    _L0_ffn_in = {k: v for k, v in _L0_ffn_all.items() if k in ('gate_w', 'shared_gate', 'shared_up', 'shared_down', 'r_gate', 'r_up', 'r_down')}
    del _L0_ffn_all

    def _L1_xattn_setup():
        import jax, jax.numpy as jnp
        import numpy as np
        IMAGE_DIM = 256
        TEXT_DIM = 192
        NUM_HEADS = 16
        HEAD_DIM = IMAGE_DIM // NUM_HEADS
        key = jax.random.key(seed)
        ks = jax.random.split(key, 14)
        B, N, M = (4, 1024, 128)
        s_img = 1.0 / np.sqrt(IMAGE_DIM)
        s_txt = 1.0 / np.sqrt(TEXT_DIM)
        s_ff = 1.0 / np.sqrt(2 * IMAGE_DIM)
        return {'x': jax.random.normal(ks[0], (B, N, IMAGE_DIM), jnp.float32), 'y': jax.random.normal(ks[1], (B, M, TEXT_DIM), jnp.float32), 'Wq': jax.random.normal(ks[2], (IMAGE_DIM, IMAGE_DIM), jnp.float32) * s_img, 'bq': jax.random.normal(ks[3], (IMAGE_DIM,), jnp.float32) * s_img, 'Wk': jax.random.normal(ks[4], (TEXT_DIM, IMAGE_DIM), jnp.float32) * s_txt, 'bk': jax.random.normal(ks[5], (IMAGE_DIM,), jnp.float32) * s_txt, 'Wv': jax.random.normal(ks[6], (TEXT_DIM, IMAGE_DIM), jnp.float32) * s_txt, 'bv': jax.random.normal(ks[7], (IMAGE_DIM,), jnp.float32) * s_txt, 'W1': jax.random.normal(ks[8], (IMAGE_DIM, 2 * IMAGE_DIM), jnp.float32) * s_img, 'b1': jax.random.normal(ks[9], (2 * IMAGE_DIM,), jnp.float32) * s_img, 'W2': jax.random.normal(ks[10], (2 * IMAGE_DIM, IMAGE_DIM), jnp.float32) * s_ff, 'b2': jax.random.normal(ks[11], (IMAGE_DIM,), jnp.float32) * s_ff}
    _L1_xattn_all = _L1_xattn_setup()
    _L1_xattn_in = {k: v for k, v in _L1_xattn_all.items() if k in ('Wq', 'bq', 'Wk', 'bk', 'Wv', 'bv', 'W1', 'b1', 'W2', 'b2')}
    del _L1_xattn_all

    def _L1_ffn_setup():
        import jax, jax.numpy as jnp
        import numpy as np
        D_MODEL = 256
        N_EXPERTS = 8
        TOP_K = 2
        LN_EPS = 1e-05
        key = jax.random.key(seed)
        ks = jax.random.split(key, 8)
        B, S, d, E = (2, 512, D_MODEL, N_EXPERTS)
        f = 2 * d
        s_in = 0.02
        return {'x': jax.random.normal(ks[0], (B, S, d), jnp.float32), 'Wg': jax.random.normal(ks[1], (d, E), jnp.float32) * s_in, 'bg': jnp.zeros((E,), jnp.float32), 'W1': jax.random.normal(ks[2], (E, d, f), jnp.float32) * s_in, 'b1': jnp.zeros((E, f), jnp.float32), 'W2': jax.random.normal(ks[3], (E, f, d), jnp.float32) * s_in, 'b2': jnp.zeros((E, d), jnp.float32), 'gamma': jnp.ones((d,), jnp.float32), 'beta': jnp.zeros((d,), jnp.float32)}
    _L1_ffn_all = _L1_ffn_setup()
    _L1_ffn_in = {k: v for k, v in _L1_ffn_all.items() if k in ('Wg', 'bg', 'W1', 'b1', 'W2', 'b2', 'gamma', 'beta')}
    del _L1_ffn_all
    return {'x': x, 'ctx_768': ctx_768, 'g_xattn': g_xattn, 'g_ffn': g_ffn, 'L0_xattn_Wq': _L0_xattn_in['Wq'], 'L0_xattn_bq': _L0_xattn_in['bq'], 'L0_xattn_Wkv': _L0_xattn_in['Wkv'], 'L0_xattn_bkv': _L0_xattn_in['bkv'], 'L0_xattn_Wo': _L0_xattn_in['Wo'], 'L0_xattn_bo': _L0_xattn_in['bo'], 'L0_ffn_gate_w': _L0_ffn_in['gate_w'], 'L0_ffn_shared_gate': _L0_ffn_in['shared_gate'], 'L0_ffn_shared_up': _L0_ffn_in['shared_up'], 'L0_ffn_shared_down': _L0_ffn_in['shared_down'], 'L0_ffn_r_gate': _L0_ffn_in['r_gate'], 'L0_ffn_r_up': _L0_ffn_in['r_up'], 'L0_ffn_r_down': _L0_ffn_in['r_down'], 'L1_xattn_Wq': _L1_xattn_in['Wq'], 'L1_xattn_bq': _L1_xattn_in['bq'], 'L1_xattn_Wk': _L1_xattn_in['Wk'], 'L1_xattn_bk': _L1_xattn_in['bk'], 'L1_xattn_Wv': _L1_xattn_in['Wv'], 'L1_xattn_bv': _L1_xattn_in['bv'], 'L1_xattn_W1': _L1_xattn_in['W1'], 'L1_xattn_b1': _L1_xattn_in['b1'], 'L1_xattn_W2': _L1_xattn_in['W2'], 'L1_xattn_b2': _L1_xattn_in['b2'], 'L1_ffn_Wg': _L1_ffn_in['Wg'], 'L1_ffn_bg': _L1_ffn_in['bg'], 'L1_ffn_W1': _L1_ffn_in['W1'], 'L1_ffn_b1': _L1_ffn_in['b1'], 'L1_ffn_W2': _L1_ffn_in['W2'], 'L1_ffn_b2': _L1_ffn_in['b2'], 'L1_ffn_gamma': _L1_ffn_in['gamma'], 'L1_ffn_beta': _L1_ffn_in['beta']}

def reference(x, ctx_768, g_xattn, g_ffn, L0_xattn_Wq, L0_xattn_bq, L0_xattn_Wkv, L0_xattn_bkv, L0_xattn_Wo, L0_xattn_bo, L0_ffn_gate_w, L0_ffn_shared_gate, L0_ffn_shared_up, L0_ffn_shared_down, L0_ffn_r_gate, L0_ffn_r_up, L0_ffn_r_down, L1_xattn_Wq, L1_xattn_bq, L1_xattn_Wk, L1_xattn_bk, L1_xattn_Wv, L1_xattn_bv, L1_xattn_W1, L1_xattn_b1, L1_xattn_W2, L1_xattn_b2, L1_ffn_Wg, L1_ffn_bg, L1_ffn_W1, L1_ffn_b1, L1_ffn_W2, L1_ffn_b2, L1_ffn_gamma, L1_ffn_beta):
    import jax
    import jax.numpy as jnp

    def _L0_xattn_ref(x, y, Wq, bq, Wkv, bkv, Wo, bo):
        import jax, jax.numpy as jnp
        import numpy as np
        N_HEADS = 16
        b, l, d = x.shape
        m = y.shape[1]
        h = N_HEADS
        dh = d // h
        q = (jnp.einsum('bld,ed->ble', x, Wq) + bq).reshape(b, l, h, dh)
        kv = (jnp.einsum('bmc,ec->bme', y, Wkv) + bkv).reshape(b, m, h, 2 * dh)
        k, v = (kv[..., :dh], kv[..., dh:])
        scale = 1.0 / jnp.sqrt(jnp.asarray(dh, x.dtype))
        att = jax.nn.softmax(jnp.einsum('blhd,bmhd->blmh', q, k) * scale, axis=2)
        out = jnp.einsum('blmh,bmhd->blhd', att, v).reshape(b, l, d)
        return jnp.einsum('bld,ed->ble', out, Wo) + bo

    def _L0_ffn_ref(hidden_states, gate_w, shared_gate, shared_up, shared_down, r_gate, r_up, r_down):
        import jax, jax.numpy as jnp
        import numpy as np
        B, S, H, F, E = (1, 512, 256, 512, 8)

        def _swiglu(x, wg, wu, wd):
            return jax.nn.silu(x @ wg.T) * (x @ wu.T) @ wd.T
        b, s, h = hidden_states.shape
        x = hidden_states.reshape(-1, h)
        shared_out = _swiglu(x, shared_gate, shared_up, shared_down)
        logits = x @ gate_w.T
        top_id = jnp.argmax(logits, axis=-1)
        score = jax.nn.sigmoid(jnp.max(logits, axis=-1))
        xs = x * score[:, None]

        def body(acc, ws):
            wg, wu, wd, e = ws
            xe = jnp.where((top_id == e)[:, None], xs, 0.0)
            return (acc + _swiglu(xe, wg, wu, wd), None)
        acc0 = jnp.zeros_like(x)
        routed_out, _ = jax.lax.scan(body, acc0, (r_gate, r_up, r_down, jnp.arange(E)))
        return (shared_out + routed_out).reshape(b, s, h)

    def _L1_xattn_ref(x, y, Wq, bq, Wk, bk, Wv, bv, W1, b1, W2, b2):
        import jax, jax.numpy as jnp
        import numpy as np
        IMAGE_DIM = 256
        TEXT_DIM = 192
        NUM_HEADS = 16
        HEAD_DIM = IMAGE_DIM // NUM_HEADS
        B, N, _ = x.shape
        M = y.shape[1]
        q = (x @ Wq + bq).reshape(B, N, NUM_HEADS, HEAD_DIM)
        k = (y @ Wk + bk).reshape(B, M, NUM_HEADS, HEAD_DIM)
        v = (y @ Wv + bv).reshape(B, M, NUM_HEADS, HEAD_DIM)
        scale = 1.0 / np.sqrt(HEAD_DIM)
        scores = jnp.einsum('bnhd,bmhd->bhnm', q, k) * scale
        attn = jax.nn.softmax(scores, axis=-1)
        out = jnp.einsum('bhnm,bmhd->bnhd', attn, v).reshape(B, N, IMAGE_DIM)
        h = jax.nn.relu(out @ W1 + b1)
        return h @ W2 + b2

    def _L1_ffn_ref(x, Wg, bg, W1, b1, W2, b2, gamma, beta):
        import jax, jax.numpy as jnp
        import numpy as np
        D_MODEL = 256
        N_EXPERTS = 8
        TOP_K = 2
        LN_EPS = 1e-05
        logits = jnp.einsum('bsd,de->bse', x, Wg) + bg
        topk_vals, topk_idx = jax.lax.top_k(logits, TOP_K)
        topk_w = jax.nn.softmax(topk_vals, axis=-1)
        h = jax.nn.relu(jnp.einsum('bsd,edf->bsef', x, W1) + b1)
        eo = jnp.einsum('bsef,efd->bsed', h, W2) + b2
        sel = jnp.take_along_axis(eo, topk_idx[..., None], axis=2)
        mixed = jnp.sum(sel * topk_w[..., None], axis=2)
        y = mixed + x
        mu = jnp.mean(y, axis=-1, keepdims=True)
        var = jnp.mean(jnp.square(y - mu), axis=-1, keepdims=True)
        return gamma * (y - mu) * jax.lax.rsqrt(var + LN_EPS) + beta
    x = x + jnp.tanh(g_xattn[0]) * _L0_xattn_ref(_layernorm(x, axis=-1), ctx_768, L0_xattn_Wq, L0_xattn_bq, L0_xattn_Wkv, L0_xattn_bkv, L0_xattn_Wo, L0_xattn_bo)
    x = x + jnp.tanh(g_ffn[0]) * _L0_ffn_ref(_layernorm(x, axis=-1), L0_ffn_gate_w, L0_ffn_shared_gate, L0_ffn_shared_up, L0_ffn_shared_down, L0_ffn_r_gate, L0_ffn_r_up, L0_ffn_r_down)
    x = x + jnp.tanh(g_xattn[1]) * _L1_xattn_ref(_layernorm(x, axis=-1), ctx_768, L1_xattn_Wq, L1_xattn_bq, L1_xattn_Wk, L1_xattn_bk, L1_xattn_Wv, L1_xattn_bv, L1_xattn_W1, L1_xattn_b1, L1_xattn_W2, L1_xattn_b2)
    x = x + jnp.tanh(g_ffn[1]) * _L1_ffn_ref(_layernorm(x, axis=-1), L1_ffn_Wg, L1_ffn_bg, L1_ffn_W1, L1_ffn_b1, L1_ffn_W2, L1_ffn_b2, L1_ffn_gamma, L1_ffn_beta)
    return x

_drawn_inputs = setup_inputs


def setup_inputs(seed=0):
    import zlib

    import numpy as np

    out = dict(_drawn_inputs(seed))
    spreads = {'g_ffn': (-1.0, 0.2),
     'L1_ffn_bg': (0.0, 0.1),
     'L1_ffn_b1': (0.0, 0.1),
     'L1_ffn_b2': (0.0, 0.1),
     'L1_ffn_gamma': (1.0, 0.2),
     'L1_ffn_beta': (0.0, 0.1)}
    factors = {'L0_xattn_bq': 5.741, 'L0_xattn_bo': 2.877, 'L1_xattn_bq': 4.734, 'L1_xattn_bk': 8.0}
    for name, (base, spread) in spreads.items():
        noise = np.random.default_rng([zlib.crc32(name.encode()), seed]).standard_normal(out[name].shape)
        drawn = base * np.exp(spread * noise) if base else spread * noise
        out[name] = jnp.asarray(drawn.astype(out[name].dtype))
    for name, factor in factors.items():
        out[name] = (out[name] * factor).astype(out[name].dtype)
    return out
```

```python
from contextlib import ExitStack

import concourse.bass as bass
from concourse import mybir

F32 = mybir.dt.float32
BF16 = mybir.dt.bfloat16
I32 = mybir.dt.int32
U32 = mybir.dt.uint32
ALU = mybir.AluOpType
ACT = mybir.ActivationFunctionType
AX = mybir.AxisListType

P = 128
S, D = 2048, 256
M, C = 1601, 192
H, DH = 16, 16
F, E = 512, 8
EPS = 1e-5
SCALE = 1.0 / DH ** 0.5

NT = S // P
KD = D // P
NC = -(-M // P)
MP = NC * P
CH = C // 2
QB = 512
NB = S // QB
TB = QB // P
HG = 4
NG = H // HG
KB = MP // 4
KLAST = M - 3 * KB
VW = 32
ROWS = 6 * DH
SHIFT = 3
STEPS = NG * NC * 2
SB = 3
KC = KB // 4
MW = (M - 1) // 4 + 1
SAFE = 40.0
QPART = [0, 0, 1, 1, 0, 2]
KPART = [0, 1, 0, 1, 2, 0]


class Layer:

    def __init__(self, n):
        self.n = n
        self.mlp = n == 1
        self.top = n + 1
        self.shared = NT if n == 0 else 0
        self.slots = self.top * NT
        self.tiles = self.shared + self.slots + E - 1
        self.tiles += 1 - self.tiles % 2
        self.experts = E + (n == 0)


def build(nc, a, out, stage=99):
    ctx = ExitStack()
    with ctx:
        def sb(name, shape, dt=F32):
            return ctx.enter_context(nc.sbuf_tensor(name, shape, dt))

        layers = [Layer(0), Layer(1)]
        parts_dram = {
            "k": [nc.dram_tensor(f"k_parts{l}", [3, D, MP], BF16).ap() for l in range(2)],
            "q": [nc.dram_tensor(f"q_parts{l}", [3, D, S], BF16).ap() for l in range(2)],
        }
        shift_dram = [nc.dram_tensor(f"shift{l}", [SHIFT, H, S], BF16).ap() for l in range(2)]
        list_x = [nc.dram_tensor(f"list_x{l.n}", [(l.tiles + 1) * P, D], F32).ap() for l in layers]
        list_y = [nc.dram_tensor(f"list_y{l.n}", [l.tiles * P, D], F32).ap() for l in layers]

        x = sb("x", [P, NT, D])
        xn = sb("xn", [P, NT, D])
        ctxT = sb("ctxT", [CH, 2, MP])
        ident = sb("ident", [P, P])
        below = sb("below", [P, P])
        ones = sb("ones", [P, P])
        pick_sum = sb("pick_sum", [P, P])
        head_rows = sb("head_rows", [P, 8], BF16)
        norms = sb("norms", [P, 8])
        top2 = sb("top2", [P, 2, 2])
        unsafe = sb("unsafe", [P, 1], I32)
        valid = sb("valid", [P, 1])
        iota8 = sb("iota8", [P, E])
        iota_tile = sb("iota_tile", [P, 48])
        gates = sb("gates", [P, 4])
        tgate = sb("tgate", [P, 4])
        wq = sb("wq", [P, KD, D])
        wk = sb("wk", [CH, 2, D])
        wv = sb("wv", [CH, 2, D])
        bq = sb("bq", [P, KD])
        bqs = sb("bqs", [P, KD])
        bk = sb("bk", [P, KD])
        bv = sb("bv", [P, D])
        w1 = sb("w1", [P, KD, 2 * D])
        b1 = sb("b1", [P, 4])
        w2 = sb("w2", [P, 4, D])
        b2 = sb("b2", [P, 2, D])
        rw = sb("rw", [P, KD, E])
        rb = sb("rb", [P, E])
        stats = sb("stats", [P, NT, 6])
        mv = sb("mv", [P, NT, 2])
        std = sb("std", [P, NT])
        rstd = sb("rstd", [P, NT])

        arena = sb("arena", [P, 28160])
        work = sb("work", [P, 5632])

        def view(region, at, shape, dt=F32):
            n = 1
            for s in shape:
                n *= s
            words = n if dt != BF16 else n // 2
            v = region[:, at:at + words]
            if dt != F32:
                v = v.bitcast(dt)
            if len(shape) == 2:
                v = v.rearrange("p (a b) -> p a b", b=shape[1])
            elif len(shape) == 3:
                v = v.rearrange("p (a b c) -> p a b c", b=shape[1], c=shape[2])
            return v, at + words

        k2, at = view(arena, 0, [H, MP], BF16)
        v_aug, at = view(arena, at, [NC, H, VW])
        q2, at = view(arena, at, [H, QB], BF16)
        probs, _ = view(arena, at, [2, HG, QB])
        xnT = [None, None]
        full = [None, None]
        for i in range(2):
            xnT[i], at = view(arena, at, [KD, QB])
            full[i], at = view(arena, at, [KD, QB])
        part = [[None] * 3, [None] * 3]
        at = 0
        for i in range(2):
            for j in range(3):
                part[i][j], at = view(work, at, [KD, QB], BF16)
        rest, at = view(work, at, [KD, QB])
        squares, at = view(work, at, [2, KD, QB], BF16)
        at = 0
        top_neg = work[:, 0:NT]
        max_full = work[0:NT, NT:NT + P]
        max_rest = work[0:NT, NT + P:NT + 2 * P]
        max_parts = [work[0:NT, NT + (4 + i) * P // 2:NT + (5 + i) * P // 2].bitcast(BF16) for i in range(SHIFT)]
        pv_sb, at = view(work, at, [QB])
        rsum, at = view(work, at, [QB])
        o_norm, at = view(work, at, [2, QB])
        oT, at = view(work, at, [KD, QB])
        hidT, at = view(work, at, [4, QB])
        y_tmp, at = view(work, at, [2 * D])
        w_gate, at = view(arena, 0, [E + 1, KD, F])
        w_up, at = view(arena, at, [E + 1, KD, F])
        w_down, at = view(arena, at, [E + 1, 4, D])
        eb1, at1 = view(arena, (E + 1) * KD * F, [E, F])
        eb2, at1 = view(arena, at1, [E, D])
        got = [view(arena, i * NT * D, [NT, D])[0] for i in range(2)]
        at = 0
        rows_in = [None] * 2
        rowsT = [None] * 2
        act_g = [None] * 2
        hid = [None] * 2
        hT = [None] * 2
        rows_out = [None] * 2
        for i in range(2):
            rows_in[i], at = view(work, at, [D])
            rowsT[i], at = view(work, at, [KD, P])
            act_g[i], at = view(work, at, [F])
            hid[i], at = view(work, at, [F])
            hT[i], at = view(work, at, [4, P])
            rows_out[i], at = view(work, at, [D])
        TS = 2 * NT
        lg = sb("lg", [P, NT, E])
        mx = sb("mx", [P, NT, 8])
        ix = sb("ix", [P, NT, 8], U32)
        ixf = sb("ixf", [P, NT, 8])
        wts = sb("wts", [P, 3, NT])
        oh = sb("oh", [P, TS, E])
        tot = sb("tot", [P, TS, E])
        scan = [sb(f"scan{i}", [P, TS, E]) for i in range(2)]
        ends = [sb(f"ends{i}", [P, E]) for i in range(2)]
        padc = sb("padc", [P, 2, E])
        padi = sb("padi", [P, 2, E], I32)
        slotf = sb("slotf", [P, TS])
        slot = sb("slot", [P, TS], U32)
        tilef = sb("tilef", [P, 48])
        tile_e = sb("tile_e", [P, 48], I32)
        gamma = sb("gamma", [P, D])
        beta = sb("beta", [P, D])

        ps = ctx.enter_context(nc.psum_tensor("ps", [P, 8, 512], F32))

        sems = {}

        def sem(name):
            if name not in sems:
                sems[name] = nc.alloc_semaphore(name)
            return sems[name]

        def free_semaphores():
            nc.clear_and_free_semaphores(list(sems.values()))
            nc.all_engine_barrier()
            sems.clear()

        class Chain:

            def __init__(self, eng, name):
                self.eng, self.sem, self.n = eng, sem(name), 0

            def __call__(self, ins):
                self.n += 1
                ins.then_inc(self.sem, 1)
                self.eng.wait_ge(self.sem, self.n)

        def spread(ap, n):
            return ap.rearrange("(a n) -> a n", a=1).broadcast_to([P, n])

        with nc.Block() as block:
            s_in, s_zero, s_set = sem("inputs_in"), sem("zeros_set"), sem("consts_set")
            s_fill, s_gate = sem("lists_filled"), sem("gates_in")

            @block.sync
            def _(sp):
                sp.dma_start(x[:, :, :], a["x"].rearrange("o (t p) d -> p (o t) d", p=P)).then_inc(s_in, 16)
                sp.wait_ge(s_zero, 1)
                for k in range(2):
                    sp.dma_start(ctxT[:, k, 0:M], a["ctxT"][k * CH:(k + 1) * CH, :]).then_inc(s_in, 16)
                for i, (name, l) in enumerate([("g_xattn", 0), ("g_ffn", 0)]):
                    sp.dma_start(gates[:, 2 * i:2 * i + 2], spread(a[name], 2)).then_inc(s_gate, 16)
                sp.wait_ge(s_zero, 2)
                for l in layers:
                    rows = list_x[l.n].rearrange("(t p) d -> p t d", p=P)
                    for t in range(l.shared, l.tiles + 1, 8):
                        n = min(8, l.tiles + 1 - t)
                        sp.dma_start(rows[:, t:t + n, :],
                                     work[:, 0:n * D].rearrange("p (t d) -> p t d", d=D)).then_inc(s_fill, 16)
                for l in range(2):
                    sp.dma_start(shift_dram[l].rearrange("r h s -> (r h) s"),
                                 work[0:SHIFT * H, 0:S // 2].bitcast(BF16)).then_inc(s_fill, 16)
                sp.wait_ge(s_in, 48)
                sp.wait_ge(s_fill, 16 * (2 + sum(-(-(l.tiles + 1 - l.shared) // 8) for l in layers)))

            @block.vector
            def _(dve):
                nc.vector.memset(ctxT[:, :, :], 0.0).then_inc(s_zero, 1)
                nc.vector.memset(work[:, 0:8 * D], 0.0).then_inc(s_zero, 1)
                nc.vector.memset(ones[:, :], 1.0).then_inc(s_set, 1)

            @block.scalar
            def _(act):
                act.wait_ge(s_gate, 32)
                nc.scalar.activation(tgate[:, :], gates[:, :], ACT.Tanh)

            @block.gpsimd
            def _(pool):
                chain = Chain(pool, "const_chain")
                chain(nc.gpsimd.memset(ident[:, :], 0.0))
                nc.gpsimd.affine_select(out=ident[:, :], in_=ident[:, :], compare_op=ALU.not_equal, fill=1.0,
                                        base=0, pattern=[[-1, P]], channel_multiplier=1)
                chain(nc.gpsimd.memset(below[:, :], 0.0))
                nc.gpsimd.affine_select(out=below[:, :], in_=below[:, :], compare_op=ALU.is_ge, fill=1.0,
                                        base=0, pattern=[[-1, P]], channel_multiplier=1)
                chain(nc.gpsimd.memset(pick_sum[:, :], 0.0))
                nc.gpsimd.affine_select(out=pick_sum[:, :].rearrange("p (b r) -> p b r", r=VW),
                                        in_=pick_sum[:, :].rearrange("p (b r) -> p b r", r=VW),
                                        compare_op=ALU.not_equal, fill=1.0, base=-DH,
                                        pattern=[[-VW, P // VW], [0, VW]], channel_multiplier=1)
                chain(nc.gpsimd.memset(head_rows[:, :], 1.0))
                chain(nc.gpsimd.affine_select(out=head_rows[:, :], in_=head_rows[:, :], compare_op=ALU.is_ge, fill=0.0,
                                              base=0, pattern=[[-DH, 8]], channel_multiplier=1))
                nc.gpsimd.affine_select(out=head_rows[:, :], in_=head_rows[:, :], compare_op=ALU.is_ge, fill=0.0,
                                        base=DH - 1, pattern=[[DH, 8]], channel_multiplier=-1)
                chain(nc.gpsimd.memset(valid[:, :], 0.0))
                nc.gpsimd.affine_select(out=valid[:, :], in_=valid[:, :], compare_op=ALU.is_ge, fill=1.0,
                                        base=-(M - (NC - 1) * P), pattern=[[0, 1]], channel_multiplier=1)
                nc.gpsimd.iota(iota8[:, :], pattern=[[1, E]], base=0, channel_multiplier=0,
                               allow_small_or_imprecise_dtypes=True)
                nc.gpsimd.iota(iota_tile[:, :], pattern=[[P, 48]], base=0, channel_multiplier=0,
                               allow_small_or_imprecise_dtypes=True)

        def layer_norm_stats(dve, chain, src, tiles, var_ready, std_ready, n):
            for t in tiles:
                last = nc.vector.bn_stats(stats[:, t, :], src[:, t, :])
            chain(last)
            for t in tiles:
                last = nc.vector.bn_aggr(mv[:, t, :], stats[:, t, :])
            chain(last)
            ts = slice(tiles[0], tiles[-1] + 1)
            nc.vector.tensor_scalar(std[:, ts], mv[:, ts, 1], EPS, None, ALU.add).then_inc(var_ready, 1)
            dve.wait_ge(std_ready, n)
            chain(nc.vector.reciprocal(rstd[:, ts], std[:, ts]))

        def take_root(act, tiles, var_ready, std_ready, n):
            act.wait_ge(var_ready, n)
            ts = slice(tiles[0], tiles[-1] + 1)
            nc.scalar.activation(std[:, ts], std[:, ts], ACT.Sqrt).then_inc(std_ready, 1)

        def normalize(dst, src, t):
            return nc.vector.tensor_scalar(dst[:, t, :], src[:, t, :], mv[:, t, 0:1], rstd[:, t:t + 1],
                                           ALU.subtract, ALU.mult)

        def attention(L):
            l = L.n
            s_var, s_rstd = sem(f"attn_var{l}"), sem(f"attn_rstd{l}")
            s_w, s_kv, s_xn = sem(f"attn_weights{l}"), sem(f"kv_weights{l}"), sem(f"xn{l}")
            s_xt, s_xtc = sem(f"xn_transposed{l}"), sem(f"xnT_copied{l}")
            s_pr, s_hi, s_sp = sem(f"projected{l}"), sem(f"high_parts{l}"), sem(f"split{l}")
            s_po = [sem(f"parts_stored{l}_{i}") for i in range(2)]
            s_v, s_va = sem(f"v_projected{l}"), sem(f"v_copied{l}")
            s_vz, s_k0, s_bqs, s_full = sem(f"v_zeroed{l}"), sem(f"k_pad{l}"), sem(f"bq_scaled{l}"), sem(f"full{l}")
            s_sq, s_nrm, s_nmx, s_top, s_all, s_uns, s_nz = (
                sem(f"squared{l}"), sem(f"norm_sums{l}"), sem(f"norm_maxima{l}"), sem(f"norm_top{l}"),
                sem(f"norm_all{l}"), sem(f"unsafe{l}"), sem(f"norms_zeroed{l}"))
            s_k2, s_q2 = sem(f"k2_in{l}"), [sem(f"q2_in{l}_{g}") for g in range(NG)]
            items = [("k", n) for n in range(4)] + [("q", b) for b in range(NB)]

            def load_q2(eng, at, g, done=None):
                cols = bass.ds(at, QB)
                for i, j in enumerate(QPART):
                    eng.dma_start(q2[i * DH:(i + 1) * DH, HG * g:HG * g + HG, :],
                                  parts_dram["q"][l][j, :, cols].rearrange("(h d) s -> d h s", d=DH)
                                  [:, HG * g:HG * g + HG, :]).then_inc(done or s_q2[g], 16)
                eng.dma_start(q2[ROWS:ROWS + SHIFT, HG * g:HG * g + HG, :],
                              shift_dram[l][:, HG * g:HG * g + HG, cols]).then_inc(done or s_q2[g], 16)

            with nc.Block() as block:
                @block.sync
                def _(sp):
                    for k in range(2):
                        sp.dma_start(wk[:, k, :], a[f"wk{l}"][k * CH:(k + 1) * CH, :]).then_inc(s_kv, 16)
                        sp.dma_start(wv[:, k, :], a[f"wv{l}"][k * CH:(k + 1) * CH, :]).then_inc(s_kv, 16)
                    sp.dma_start(bk[:, :], a[f"bk{l}"]).then_inc(s_kv, 16)
                    sp.dma_start(bv[:, :], spread(a[f"bv{l}"], D)).then_inc(s_kv, 16)
                    sp.dma_start(wq[:, :, :], a[f"wq{l}"].rearrange("(k p) n -> p k n", p=P)).then_inc(s_kv, 16)
                    sp.dma_start(bq[:, :], a[f"bq{l}"]).then_inc(s_kv, 16)
                    if L.mlp:
                        sp.dma_start(w1[:, :, :], a["w1"].rearrange("(k p) n -> p k n", p=P)).then_inc(s_w, 16)
                        sp.dma_start(b1[:, :], a["b1"]).then_inc(s_w, 16)
                        sp.dma_start(w2[:, :, :], a["w2"].rearrange("(k p) n -> p k n", p=P)).then_inc(s_w, 16)
                    else:
                        sp.dma_start(w2[:, 0:KD, :], a["wo"].rearrange("(k p) n -> p k n", p=P)).then_inc(s_w, 16)
                    for i in range(2):
                        sp.dma_start(b2[:, i, :], spread(a[f"bo{l}"], D)).then_inc(s_w, 16)
                    for n, (kind, b) in enumerate(items):
                        w = KB if kind == "k" else QB
                        sp.wait_ge(s_sp, n + 1)
                        for j in range(3):
                            sp.dma_start(parts_dram[kind][l][j, :, b * w:(b + 1) * w]
                                         .rearrange("(k p) s -> p k s", p=P),
                                         part[n % 2][j][:, :, 0:w]).then_inc(s_po[n % 2], 16)
                        if n == 3:
                            for i in range(2):
                                sp.wait_ge(s_po[i], 96)
                            for i, j in enumerate(KPART):
                                sp.dma_start(k2[i * DH:(i + 1) * DH, :, :],
                                             parts_dram["k"][l][j].rearrange("(h d) s -> d h s", d=DH)
                                             ).then_inc(s_k2, 16)
                        if n == 5:
                            sp.wait_ge(s_po[0], 144)
                            for g in range(NG):
                                load_q2(sp, 0, g)
                    sp.wait_ge(s_k2, 96)
                    for g in range(NG):
                        sp.wait_ge(s_q2[g], 16 * 7)
                    sp.wait_ge(s_po[0], 192)
                    sp.wait_ge(s_po[1], 192)
                    sp.wait_ge(s_w, 16 * (5 if L.mlp else 3))

                @block.scalar
                def _(act):
                    take_root(act, range(NT), s_var, s_rstd, 1)
                    act.wait_ge(s_kv, 128)
                    nc.scalar.activation(bqs[:, :], bq[:, :], ACT.Copy, scale=SCALE).then_inc(s_bqs, 1)
                    act.wait_ge(s_bqs, 1)
                    for n, (kind, b) in enumerate(items):
                        w = KB if kind == "k" else QB
                        if kind == "k" and b == 3:
                            w = KLAST
                        if kind == "q":
                            act.wait_ge(s_xt, b + 1)
                            nc.scalar.activation(xnT[b % 2], ps[:, 2 * (b % 2):2 * (b % 2) + 2, :],
                                                 ACT.Copy).then_inc(s_xtc, 1)
                        bank = 4 + 2 * (n % 2)
                        bias = bk if kind == "k" else bqs
                        scale = 1.0 if kind == "k" else SCALE
                        act.wait_ge(s_pr, n + 1)
                        if n >= 2:
                            act.wait_ge(s_sp, n - 1)
                            act.wait_ge(s_sq, n - 1)
                            act.wait_ge(s_po[n % 2], 48 * (n // 2))
                        for k in range(KD):
                            nc.scalar.activation(full[n % 2][:, k, 0:w], ps[:, bank + k, 0:w], ACT.Identity,
                                                 bias=bias[:, k:k + 1], scale=scale).then_inc(s_full, 1)
                            last = nc.scalar.activation(part[n % 2][0][:, k, 0:w], ps[:, bank + k, 0:w],
                                                        ACT.Identity, bias=bias[:, k:k + 1], scale=scale)
                            last.then_inc(s_hi, 1)

                @block.tensor
                def _(pe):
                    pe.wait_ge(s_kv, 128)

                    def transpose_block(b):
                        pe.wait_ge(s_xn, b + 1)
                        for t in range(TB):
                            for k in range(KD):
                                last = nc.tensor.transpose(ps[:, 2 * (b % 2) + k, t * P:(t + 1) * P],
                                                           xn[:, b * TB + t, k * P:(k + 1) * P], ident[:, :])
                        last.then_inc(s_xt, 1)

                    def norm(n):
                        pe.wait_ge(s_sq, n + 1)
                        c = KC if items[n][0] == "k" else P
                        for t in range(4):
                            for k in range(KD):
                                at = (t * KD + k) * 8
                                last = nc.tensor.matmul(ps[0:c, 4 + 2 * (n % 2), at:at + 8],
                                                        squares[:, n % 2, k, t * c:(t + 1) * c], head_rows[:, :],
                                                        start=True, stop=True)
                        last.then_inc(s_nrm, 1)

                    for n, (kind, b) in enumerate(items):
                        bank = 4 + 2 * (n % 2)
                        if n == 3:
                            transpose_block(0)
                        if kind == "q" and b + 1 < NB:
                            if b >= 1:
                                pe.wait_ge(s_xtc, b)
                            transpose_block(b + 1)
                        if kind == "q":
                            pe.wait_ge(s_xtc, b + 1)
                        if n >= 2:
                            pe.wait_ge(s_nmx, n - 1)
                        for ko in range(KD):
                            for ki in range(2):
                                if kind == "k":
                                    w = KB if b < 3 else KLAST
                                    last = nc.tensor.matmul(ps[:, bank + ko, 0:w], wk[:, ki, ko * P:(ko + 1) * P],
                                                            ctxT[:, ki, b * KB:b * KB + w],
                                                            start=(ki == 0), stop=(ki == 1))
                                else:
                                    last = nc.tensor.matmul(ps[:, bank + ko, :], wq[:, ki, ko * P:(ko + 1) * P],
                                                            xnT[b % 2][:, ki, :], start=(ki == 0), stop=(ki == 1))
                        last.then_inc(s_pr, 1)
                        if n >= 1:
                            norm(n - 1)
                    norm(len(items) - 1)
                    for c in range(NC):
                        bank = c % 4
                        if c == 0:
                            pe.wait_ge(s_xtc, NB)
                        if c >= 4:
                            pe.wait_ge(s_va, c - 3)
                        for ki in range(2):
                            last = nc.tensor.matmul(ps[:, bank, 0:D], ctxT[:, ki, c * P:(c + 1) * P], wv[:, ki, :],
                                                    start=(ki == 0), stop=(ki == 1))
                        last.then_inc(s_v, 1)

                @block.vector
                def _(dve):
                    chain = Chain(dve, f"prep_chain{l}")
                    chain(nc.vector.memset(norms[:, :], 0.0))
                    layer_norm_stats(dve, chain, x, range(NT), s_var, s_rstd, 1)
                    for t in range(NT):
                        last = normalize(xn, x, t)
                        if t % TB == TB - 1:
                            last.then_inc(s_xn, 1)
                    for n, (kind, b) in enumerate(items):
                        w = KB if kind == "k" else QB
                        i = n % 2
                        if kind == "k" and b == 3:
                            w = KLAST
                        dve.wait_ge(s_hi, KD * (n + 1))
                        chain(nc.vector.tensor_tensor(rest[:, :, 0:w], full[i][:, :, 0:w], part[i][0][:, :, 0:w],
                                                      ALU.subtract))
                        chain(nc.vector.tensor_copy(part[i][1][:, :, 0:w], rest[:, :, 0:w]))
                        if w == KLAST:
                            for j in range(3):
                                chain(nc.vector.memset(part[i][j][:, :, w:KB], 0.0))
                        nc.vector.tensor_tensor(part[i][2][:, :, 0:w], rest[:, :, 0:w], part[i][1][:, :, 0:w],
                                                ALU.subtract).then_inc(s_sp, 1)
                        dve.wait_ge(s_sp, n + 1)
                        dve.wait_ge(s_nrm, n + 1)
                        c = KC if kind == "k" else P
                        nc.vector.tensor_reduce(norms[0:c, n:n + 1], ps[0:c, 4 + 2 * i, 0:8 * 8], AX.X, ALU.max
                                                ).then_inc(s_nmx, 1)
                    dve.wait_ge(s_nmx, len(items))
                    nc.vector.tensor_reduce(top2[:, 0, :], norms[:, :].rearrange("p (a b) -> p a b", a=2), AX.X,
                                            ALU.max).then_inc(s_top, 1)
                    for c in range(NC):
                        if c == 0:
                            dve.wait_ge(s_vz, 1)
                        dve.wait_ge(s_v, c + 1)
                        last = nc.vector.tensor_tensor(
                            v_aug[:, c, :, 0:DH], ps[:, c % 4, 0:D].rearrange("p (h d) -> p h d", d=DH),
                            bv[:, :].rearrange("p (h d) -> p h d", d=DH), ALU.add)
                        last.then_inc(s_va, 1)
                    dve.wait_ge(s_va, NC)
                    chain(nc.vector.tensor_scalar(v_aug[:, NC - 1, :, :], v_aug[:, NC - 1, :, :],
                                                  valid[:, 0:1], None, ALU.mult))
                    dve.wait_ge(s_all, 1)
                    chain(nc.vector.tensor_tensor(top2[:, 0, 0:1], top2[:, 1, 0:1], top2[:, 1, 1:2], ALU.mult))
                    chain(nc.vector.tensor_scalar(unsafe[:, :], top2[:, 0, 0:1], SAFE * SAFE, None, ALU.is_gt))

                @block.gpsimd
                def _(pool):
                    chain = Chain(pool, f"fill_chain{l}")
                    chain(nc.gpsimd.memset(v_aug, 0.0))
                    nc.gpsimd.memset(v_aug[:, :, :, DH:DH + 1], 1.0).then_inc(s_vz, 1)
                    pool.wait_ge(s_vz, 1)
                    chain(nc.gpsimd.memset(k2[ROWS:P, :, :], 0.0))
                    chain(nc.gpsimd.memset(k2[ROWS:ROWS + SHIFT, :, 0:M], 1.0))
                    for n, (kind, b) in enumerate(items):
                        i, w = n % 2, KB if kind == "k" else QB
                        if n == 3:
                            w = KLAST
                            pool.wait_ge(s_nrm, n - 1)
                            chain(nc.gpsimd.memset(squares[:, i, :, KLAST:KB], 0.0))
                        elif n >= 2:
                            pool.wait_ge(s_nrm, n - 1)
                        pool.wait_ge(s_full, KD * (n + 1))
                        nc.gpsimd.tensor_tensor(squares[:, i, :, 0:w], full[i][:, :, 0:w], full[i][:, :, 0:w],
                                                ALU.mult).then_inc(s_sq, 1)
                    pool.wait_ge(s_top, 1)
                    nc.gpsimd.partition_all_reduce(top2[:, 1, :], top2[:, 0, :], P, bass.bass_isa.ReduceOp.max
                                                   ).then_inc(s_all, 1)

            s_hq, s_ms, s_mm, s_mt, s_mc, s_mo, s_md = (
                sem(f"head_q{l}"), sem(f"max_scores{l}"), sem(f"max_taken{l}"), sem(f"max_turned{l}"),
                sem(f"max_copied{l}"), sem(f"max_split{l}"), sem(f"shift_stored{l}"))
            s_m1, s_m2, s_m3 = [sem(f"max_part{l}_{i}") for i in range(3)]
            s_re = sem(f"q2_again{l}")
            q_head = q2.rearrange("p h s -> p (h s)")[:, 0:S]
            with nc.Block() as block:
                def asked(eng):
                    return eng.If(eng.value_load(unsafe[0:1, 0:1], min_val=0, max_val=1) > 0)

                @block.sync
                def _(sp):
                    with asked(sp):
                        def load_head(h):
                            for i, j in enumerate(QPART):
                                sp.dma_start(q_head[i * DH:(i + 1) * DH, :],
                                             parts_dram["q"][l][j].rearrange("(h d) s -> h d s", d=DH)
                                             [bass.ds(h, 1), :, :].rearrange("a d s -> (a d) s")
                                             ).then_inc(s_hq, 16)

                        def store_head(h):
                            sp.wait_ge(s_mo, h + 1)
                            for j in range(SHIFT):
                                sp.dma_start(shift_dram[l][j, bass.ds(h, 1), :]
                                             .rearrange("a (t q) -> (a t) q", q=P), max_parts[j]).then_inc(s_md, 16)

                        load_head(0)
                        store_head(0)
                        with sp.Fori(1, H) as h:
                            load_head(h)
                            store_head(h)
                        sp.wait_ge(s_md, 16 * SHIFT * H)
                        for g in range(NG):
                            load_q2(sp, 0, g, s_re)
                        sp.wait_ge(s_re, 16 * 7 * NG)

                @block.tensor
                def _(pe):
                    with asked(pe):
                        def head(h, first):
                            pe.wait_ge(s_hq, 96 if first else h * 96 + 96)
                            for t in range(NT):
                                bank = 4 * (t % 2)
                                if t >= 2:
                                    pe.wait_ge(s_mm, t - 1 if first else h * NT + t - 1)
                                for i in range(4):
                                    last = nc.tensor.matmul(
                                        ps[:, bank + i, 0:MW], q_head[0:ROWS, t * P:(t + 1) * P],
                                        k2[0:ROWS, bass.ds(h, 1), i * (MW - 1):i * (MW - 1) + MW]
                                        .rearrange("p a n -> p (a n)"), start=True, stop=True)
                                last.then_inc(s_ms, 1)
                            pe.wait_ge(s_mm, NT if first else h * NT + NT)
                            nc.tensor.transpose(ps[0:NT, 0, 0:P], top_neg, ident[:, :]).then_inc(s_mt, 1)
                            pe.wait_ge(s_mc, 1 if first else h + 1)
                        head(0, True)
                        with pe.Fori(1, H) as h:
                            head(h, False)

                @block.vector
                def _(dve):
                    with asked(dve):
                        def head(h, first):
                            for t in range(NT):
                                dve.wait_ge(s_ms, t + 1 if first else h * NT + t + 1)
                                nc.vector.tensor_reduce(top_neg[:, t:t + 1], ps[:, 4 * (t % 2):4 * (t % 2) + 4, 0:MW],
                                                        AX.XY, ALU.max, negate=True).then_inc(s_mm, 1)
                            dve.wait_ge(s_mt, 1 if first else h + 1)
                            nc.vector.tensor_copy(max_full, ps[0:NT, 0, 0:P]).then_inc(s_mc, 1)
                            dve.wait_ge(s_mc, 1 if first else h + 1)
                            if not first:
                                dve.wait_ge(s_md, h * 16 * SHIFT)
                            nc.vector.tensor_copy(max_parts[0], max_full).then_inc(s_m1, 1)
                            dve.wait_ge(s_m1, 1 if first else h + 1)
                            nc.vector.tensor_tensor(max_rest, max_full, max_parts[0], ALU.subtract).then_inc(s_m2, 1)
                            dve.wait_ge(s_m2, 1 if first else h + 1)
                            nc.vector.tensor_copy(max_parts[1], max_rest).then_inc(s_m3, 1)
                            dve.wait_ge(s_m3, 1 if first else h + 1)
                            nc.vector.tensor_tensor(max_parts[2], max_rest, max_parts[1], ALU.subtract
                                                    ).then_inc(s_mo, 1)
                        head(0, True)
                        with dve.Fori(1, H) as h:
                            head(h, False)

            s_qk, s_exp, s_pv, s_u = sem(f"scores{l}"), sem(f"exps{l}"), sem(f"pv{l}"), sem(f"pv_copied{l}")
            s_full7, s_read7 = sem(f"bank7_full{l}"), sem(f"bank7_read{l}")
            s_on, s_oc = sem(f"o_normed{l}"), [sem(f"oT_in{l}_{i}") for i in range(2)]
            s_xup = [sem(f"x_updated{l}_{i}") for i in range(2)]
            NU = NG + 2 + (4 if L.mlp else 0)

            def use(b, k):
                return (b - 1) * NU + NG - 1 + k + 1

            with nc.Block() as block:
                @block.tensor
                def _(pe):
                    def scores(b, w):
                        g, c = divmod(w, NC)
                        if c == 0:
                            pe.wait_ge(s_q2[g], (b + 1) * 16 * 7)
                        for half in range(2):
                            u = 2 * w + half
                            buf = 2 * (u % SB)
                            last_read = u - SB if u >= SB else max(v for v in range(STEPS) if v % SB == u % SB) - STEPS
                            if not (isinstance(b, int) and b == 0 and u < SB):
                                pe.wait_ge(s_exp, b * STEPS + last_read + 1)
                            for j in range(2):
                                h = HG * g + 2 * half + j
                                last = nc.tensor.matmul(ps[:, buf + j, :], k2[0:ROWS + SHIFT, h, c * P:(c + 1) * P],
                                                        q2[0:ROWS + SHIFT, h, :], start=True, stop=True)
                            last.then_inc(s_qk, 1)

                    def weigh(b, w):
                        g, c = divmod(w, NC)
                        pe.wait_ge(s_exp, b * STEPS + 2 * w + 2)
                        if c == 0 and not (isinstance(b, int) and b == 0 and g == 0):
                            pe.wait_ge(s_u, b * NG + g)
                        for j in range(HG):
                            last = nc.tensor.matmul(ps[j * VW:(j + 1) * VW, 6, :], v_aug[:, c, HG * g + j, :],
                                                    probs[:, w % 2, j, :], start=(c == 0), stop=(c == NC - 1),
                                                    skip_group_check=True)
                        last.then_inc(s_pv, 1)

                    def sums(b, g, n):
                        pe.wait_ge(s_u, b * NG + g + 1)
                        if not (isinstance(n, int) and n == 1):
                            pe.wait_ge(s_read7, n - 1)
                        nc.tensor.matmul(ps[:, 7, :], pick_sum[:, :], pv_sb, start=True, stop=True
                                         ).then_inc(s_full7, 1)

                    def hidden(b, f, n):
                        if f == 0:
                            for i in range(2):
                                pe.wait_ge(s_oc[i], (b + 1) * 16 * HG * NG // 2)
                        pe.wait_ge(s_read7, n - 1)
                        for k in range(KD):
                            last = nc.tensor.matmul(ps[:, 7, :], w1[:, k, f * P:(f + 1) * P], oT[:, k, :],
                                                    start=(k == 0), stop=(k == KD - 1))
                        last.then_inc(s_full7, 1)

                    def output(b, pair, half, n):
                        if half == 0:
                            for i in range(2):
                                pe.wait_ge(s_oc[i], (b + 1) * 16 * HG * NG // 2)
                            pe.wait_ge(s_read7, n - 1)
                        src, ks = (hidT, 4) if L.mlp else (oT, KD)
                        t = 2 * pair + half
                        for k in range(ks):
                            last = nc.tensor.matmul(ps[:, 7, half * D:(half + 1) * D], src[:, k, t * P:(t + 1) * P],
                                                    w2[:, k, :], start=(k == 0), stop=(k == ks - 1),
                                                    skip_group_check=True)
                        if half == 1:
                            last.then_inc(s_full7, 1)

                    def tail_items(b, now):
                        items = [(3, lambda: sums(now, NG - 1, use(b, 0)))]
                        k, at = 1, 6
                        if L.mlp:
                            for f in range(4):
                                items.append((at, lambda f=f, k=k: hidden(now, f, use(b, k))))
                                k, at = k + 1, at + 1
                        for pair in range(2):
                            for half in range(2):
                                items.append((at, lambda p=pair, h=half, k=k: output(now, p, h, use(b, k))))
                                at += 1
                            k += 1
                        return items

                    def body(b, first):
                        items = [] if first else tail_items(b, b - 1)
                        k0 = 1 + NU - NG
                        for g in range(NG - 1):
                            n = g + 1 if first else use(b, k0 + g)
                            items.append((NC * (g + 1) + 3, lambda g=g, n=n: sums(b, g, n)))
                        for w in range(NG * NC):
                            scores(b, w)
                            if w > 0:
                                weigh(b, w - 1)
                            elif not first:
                                weigh(b - 1, NG * NC - 1)
                            for at, work_item in items:
                                if at == w:
                                    work_item()

                    body(0, True)
                    with pe.Fori(1, NB) as b:
                        body(b, False)
                    weigh(NB - 1, NG * NC - 1)
                    for _, work_item in tail_items(NB, NB - 1):
                        work_item()

                @block.scalar
                def _(act):
                    def body(b, first):
                        for u in range(STEPS):
                            w, half = divmod(u, 2)
                            buf = 2 * (u % SB)
                            act.wait_ge(s_qk, b * STEPS + u + 1)
                            if half == 0 and not (first and w < 2):
                                act.wait_ge(s_pv, b * NG * NC + w - 1)
                            nc.scalar.activation(probs[:, w % 2, 2 * half:2 * half + 2, :], ps[:, buf:buf + 2, :],
                                                 ACT.Exp).then_inc(s_exp, 1)
                    body(0, True)
                    with act.Fori(1, NB) as b:
                        body(b, False)

                @block.vector
                def _(dve):
                    tg = tgate[:, l:l + 1]

                    def group(b, g, n):
                        dve.wait_ge(s_pv, b * NG * NC + NC * (g + 1))
                        nc.vector.tensor_copy(pv_sb, ps[:, 6, :]).then_inc(s_u, 1)
                        dve.wait_ge(s_full7, n)
                        nc.vector.reciprocal(rsum, ps[:, 7, :]).then_inc(s_read7, 1)
                        dve.wait_ge(s_read7, n)
                        if g >= 2 or not (isinstance(b, int) and b == 0):
                            dve.wait_ge(s_oc[g % 2], (b * (NG // 2) + g // 2) * 16 * HG)
                        nc.vector.tensor_tensor(o_norm[:, g % 2, :], pv_sb, rsum, ALU.mult).then_inc(s_on, 1)
                        dve.wait_ge(s_on, b * NG + g + 1)

                    def tail(b, now):
                        group(now, NG - 1, use(b, 0))
                        k = 1
                        if L.mlp:
                            for f in range(4):
                                dve.wait_ge(s_full7, use(b, k))
                                nc.vector.tensor_scalar(hidT[:, f, :], ps[:, 7, :], b1[:, f:f + 1], 0.0,
                                                        ALU.add, ALU.max).then_inc(s_read7, 1)
                                k += 1
                        for pair in range(2):
                            dve.wait_ge(s_full7, use(b, k))
                            nc.vector.tensor_tensor(y_tmp.rearrange("p (t d) -> p t d", d=D),
                                                    ps[:, 7, :].rearrange("p (t d) -> p t d", d=D), b2[:, :, :],
                                                    ALU.add).then_inc(s_read7, 1)
                            dve.wait_ge(s_read7, use(b, k))
                            rows = x[:, bass.ds(now * TB + 2 * pair, 2), :]
                            nc.vector.scalar_tensor_tensor(out=rows, in0=y_tmp.rearrange("p (t d) -> p t d", d=D),
                                                           scalar=tg, in1=rows, op0=ALU.mult,
                                                           op1=ALU.add).then_inc(s_xup[pair], 1)
                            dve.wait_ge(s_xup[pair], now + 1)
                            k += 1

                    def body(b, first):
                        if not first:
                            tail(b, b - 1)
                        for g in range(NG - 1):
                            group(b, g, g + 1 if first else use(b, 1 + NU - NG + g))
                    body(0, True)
                    with dve.Fori(1, NB) as b:
                        body(b, False)
                    tail(NB, NB - 1)

                @block.sync
                def _(sp):
                    def gather_heads(b, g):
                        later = g == 0 and not (isinstance(b, int) and b == 0)
                        sp.wait_ge(s_on, b * NG + g + 1)
                        if later:
                            sp.wait_ge(s_xup[1], b)
                        for j in range(HG):
                            h = HG * g + j
                            sp.dma_start(oT[(h % 8) * DH:(h % 8 + 1) * DH, h // 8, :],
                                         o_norm[j * VW:j * VW + DH, g % 2, :]).then_inc(s_oc[g % 2], 16)

                    def body(b, first):
                        if not first:
                            gather_heads(b - 1, NG - 1)
                        at = QB if first else sp.snap((b + 1) % NB * QB)
                        for g in range(NG):
                            sp.wait_ge(s_qk, b * STEPS + 2 * NC * (g + 1))
                            load_q2(sp, at, g)
                            if g < NG - 1:
                                gather_heads(b, g)
                    body(0, True)
                    with sp.Fori(1, NB) as b:
                        body(b, False)
                    gather_heads(NB - 1, NG - 1)
                    for g in range(NG):
                        sp.wait_ge(s_q2[g], (NB + 1) * 16 * 7)

        def moe(L):
            l = L.n
            NTL, T = L.tiles, L.slots
            s_var, s_rstd = sem(f"moe_var{l}"), sem(f"moe_rstd{l}")
            s_w, s_e = sem(f"router_in{l}"), [sem(f"expert_in{l}_{e}") for e in range(L.experts)]
            s_xn, s_xt, s_xtc = sem(f"moe_xn{l}"), sem(f"moe_xT{l}"), sem(f"moe_xTc{l}")
            s_lg, s_oh, s_cnt, s_slot = sem(f"logits{l}"), sem(f"onehot{l}"), sem(f"counts{l}"), sem(f"slots{l}")
            s_mx, s_ex, s_send, s_sh, s_xs = (sem(f"tops{l}"), sem(f"top_exp{l}"), sem(f"rows_sent{l}"),
                                              sem(f"shared_sent{l}"), sem(f"rows_scaled{l}"))

            def load_expert(eng, e):
                if l == 0:
                    src = (("sg", "su", "sd") if e == E else ("rg", "ru", "rd"))
                    for dst, name in zip((w_gate, w_up, w_down), src):
                        w = a[name] if e == E else a[name][e]
                        eng.dma_start(dst[:, e, :, :], w.rearrange("(k p) n -> p k n", p=P)).then_inc(s_e[e], 16)
                else:
                    eng.dma_start(w_gate[:, e, :, :], a["ew1"][e].rearrange("(k p) n -> p k n", p=P)).then_inc(s_e[e], 16)
                    eng.dma_start(w_down[:, e, :, :], a["ew2"][e].rearrange("(k p) n -> p k n", p=P)).then_inc(s_e[e], 16)
                    eng.dma_start(eb1[:, e, :], spread(a["eb1"][e], F)).then_inc(s_e[e], 16)
                    eng.dma_start(eb2[:, e, :], spread(a["eb2"][e], D)).then_inc(s_e[e], 16)

            rxT = [view(work, i * KD * QB, [KD, QB])[0] for i in range(2)]

            with nc.Block() as block:
                @block.sync
                def _(sp):
                    sp.dma_start(rw[:, :, :], a[f"rw{l}"].rearrange("(k p) n -> p k n", p=P)).then_inc(s_w, 16)
                    if l == 1:
                        sp.dma_start(rb[:, :], spread(a["rb1"], E)).then_inc(s_w, 16)
                        sp.dma_start(gamma[:, :], spread(a["gamma"], D)).then_inc(s_w, 16)
                        sp.dma_start(beta[:, :], spread(a["beta"], D)).then_inc(s_w, 16)
                    for e in ([E] if l == 0 else []) + list(range(E)):
                        load_expert(sp, e)
                    if l == 0:
                        sp.wait_ge(s_xn, 4)
                        sp.dma_start(list_x[0][0:S, :].rearrange("(t p) d -> p t d", p=P), xn[:, :, :]
                                     ).then_inc(s_sh, 16)
                    for q in s_e:
                        sp.wait_ge(q, 16 * (3 if l == 0 else 4))

                @block.tensor
                def _(pe):
                    pe.wait_ge(s_w, 16 if l == 0 else 64)

                    def logits(b):
                        pe.wait_ge(s_xtc, b + 1)
                        for t in range(TB):
                            n = b * TB + t
                            for k in range(KD):
                                last = nc.tensor.matmul(ps[:, 4, n * E:(n + 1) * E],
                                                        rxT[b % 2][:, k, t * P:(t + 1) * P], rw[:, k, :],
                                                        start=(k == 0), stop=(k == KD - 1), skip_group_check=True)
                        if b == NB - 1:
                            last.then_inc(s_lg, 1)

                    for b in range(NB):
                        pe.wait_ge(s_xn, b + 1)
                        for t in range(TB):
                            for k in range(KD):
                                last = nc.tensor.transpose(ps[:, 2 * (b % 2) + k, t * P:(t + 1) * P],
                                                           xn[:, b * TB + t, k * P:(k + 1) * P], ident[:, :])
                        last.then_inc(s_xt, 1)
                        if b:
                            logits(b - 1)
                    logits(NB - 1)
                    pe.wait_ge(s_oh, 1)
                    nc.tensor.matmul(ps[:, 5, 0:T * E], below[:, :], oh[:, 0:T, :], start=True, stop=True)
                    nc.tensor.matmul(ps[:, 6, 0:T * E], ones[:, :], oh[:, 0:T, :], start=True, stop=True
                                     ).then_inc(s_cnt, 1)

                @block.scalar
                def _(act):
                    take_root(act, range(NT), s_var, s_rstd, 1)
                    for b in range(NB):
                        act.wait_ge(s_xt, b + 1)
                        nc.scalar.activation(rxT[b % 2], ps[:, 2 * (b % 2):2 * (b % 2) + 2, :],
                                             ACT.Copy).then_inc(s_xtc, 1)
                    act.wait_ge(s_mx, 1)
                    if l == 0:
                        nc.scalar.activation(wts[:, 0, :], mx[:, :, 0], ACT.Exp, scale=-1.0).then_inc(s_ex, 1)
                    else:
                        nc.scalar.activation(wts[:, 0, :], wts[:, 2, :], ACT.Exp).then_inc(s_ex, 1)

                @block.vector
                def _(dve):
                    chain = Chain(dve, f"route_chain{l}")
                    layer_norm_stats(dve, chain, x, range(NT), s_var, s_rstd, 1)
                    for t in range(NT):
                        last = normalize(xn, x, t)
                        if t % TB == TB - 1:
                            last.then_inc(s_xn, 1)
                    dve.wait_ge(s_lg, 1)
                    logit_ps = ps[:, 4, 0:NT * E].rearrange("p (t e) -> p t e", e=E)
                    if l == 0:
                        chain(nc.vector.tensor_copy(lg[:, :, :], logit_ps))
                    else:
                        chain(nc.vector.tensor_tensor(lg[:, :, :], logit_ps,
                                                      rb[:, :].unsqueeze(1).broadcast_to([P, NT, E]), ALU.add))
                    for t in range(NT):
                        last = nc.vector.max(mx[:, t, :], lg[:, t, :])
                    chain(last)
                    for t in range(NT):
                        last = nc.vector.max_index(ix[:, t, :], mx[:, t, :], lg[:, t, :])
                    chain(last)
                    if l == 1:
                        chain(nc.vector.tensor_tensor(wts[:, 2, :], mx[:, :, 1], mx[:, :, 0], ALU.subtract))
                    chain(nc.vector.tensor_copy(ixf[:, :, :], ix[:, :, :]))
                    for i in range(T):
                        last = nc.vector.tensor_scalar(oh[:, i, :], iota8[:, :], ixf[:, i % NT, i // NT:i // NT + 1],
                                                       None, ALU.is_equal)
                        if i == 0:
                            last.then_inc(s_mx, 1)
                    last.then_inc(s_oh, 1)
                    dve.wait_ge(s_ex, 1)
                    chain(nc.vector.tensor_scalar(wts[:, 1, :], wts[:, 0, :], 1.0, None, ALU.add))
                    chain(nc.vector.reciprocal(wts[:, 2, :], wts[:, 1, :]))
                    if l == 1:
                        chain(nc.vector.tensor_tensor(wts[:, 1, :], wts[:, 0, :], wts[:, 2, :], ALU.mult))
                    else:
                        dve.wait_ge(s_sh, 16)
                        for t in range(NT):
                            last = nc.vector.tensor_scalar(xn[:, t, :], xn[:, t, :], wts[:, 2, t:t + 1], None, ALU.mult)
                        last.then_inc(s_xs, 1)
                    dve.wait_ge(s_cnt, 1)
                    before = ps[:, 5, 0:T * E].rearrange("p (t e) -> p t e", e=E)
                    tots = ps[:, 6, 0:T * E].rearrange("p (t e) -> p t e", e=E)
                    chain(nc.vector.tensor_copy(tot[:, 0:T, :], tots))
                    chain(nc.vector.tensor_copy(scan[0][:, 0:T, :], tots))
                    i, step = 0, 1
                    while step < T:
                        nc.vector.tensor_copy(scan[1 - i][:, 0:step, :], scan[i][:, 0:step, :])
                        chain(nc.vector.tensor_tensor(scan[1 - i][:, step:T, :], scan[i][:, step:T, :],
                                                      scan[i][:, 0:T - step, :], ALU.add))
                        i, step = 1 - i, 2 * step
                    incl, other = scan[i], scan[1 - i]
                    chain(nc.vector.tensor_scalar(padi[:, 0, :], incl[:, T - 1, :], float(P - 1), None, ALU.add))
                    chain(nc.vector.tensor_scalar(padi[:, 1, :], padi[:, 0, :], 7, 7, ALU.logical_shift_right,
                                                  ALU.logical_shift_left))
                    chain(nc.vector.tensor_copy(padc[:, 0, :], padi[:, 1, :]))
                    chain(nc.vector.tensor_copy(ends[0][:, :], padc[:, 0, :]))
                    j, step = 0, 1
                    while step < E:
                        nc.vector.tensor_copy(ends[1 - j][:, 0:step], ends[j][:, 0:step])
                        chain(nc.vector.tensor_tensor(ends[1 - j][:, step:E], ends[j][:, step:E],
                                                      ends[j][:, 0:E - step], ALU.add))
                        j, step = 1 - j, 2 * step
                    end = ends[j]
                    chain(nc.vector.tensor_tensor(padc[:, 1, :], end[:, :], padc[:, 0, :], ALU.subtract))
                    chain(nc.vector.tensor_tensor(other[:, 0:T, :], incl[:, 0:T, :], tot[:, 0:T, :], ALU.subtract))
                    chain(nc.vector.tensor_tensor(incl[:, 0:T, :], before, other[:, 0:T, :], ALU.add))
                    chain(nc.vector.tensor_tensor(other[:, 0:T, :], incl[:, 0:T, :],
                                                  padc[:, 1, :].unsqueeze(1).broadcast_to([P, T, E]), ALU.add))
                    chain(nc.vector.tensor_tensor(incl[:, 0:T, :], other[:, 0:T, :], oh[:, 0:T, :], ALU.mult))
                    chain(nc.vector.tensor_reduce(slotf[:, 0:T], incl[:, 0:T, :], AX.X, ALU.add))
                    nc.vector.tensor_scalar(slot[:, 0:T], slotf[:, 0:T], float(L.shared * P), None, ALU.add
                                            ).then_inc(s_slot, 1)
                    routed = NTL - L.shared
                    chain(nc.vector.memset(tilef[:, :], float(E)))
                    tv = tilef[:, L.shared:NTL]
                    chain(nc.vector.memset(tv, 0.0))
                    for e in range(E - 1):
                        chain(nc.vector.scalar_tensor_tensor(out=tv, in0=iota_tile[:, 0:routed], scalar=end[:, e:e + 1],
                                                             in1=tv, op0=ALU.is_ge, op1=ALU.add))
                    chain(nc.vector.tensor_copy(tile_e[:, :], tilef[:, :]))

                @block.gpsimd
                def _(pool):
                    pool.wait_ge(s_slot, 1)
                    if l == 0:
                        pool.wait_ge(s_xs, 1)
                    for i in range(T):
                        nc.gpsimd.indirect_dma_start(
                            out=list_x[l], out_offset=bass.IndirectOffsetOnAxis(ap=slot[:, i:i + 1], axis=0),
                            in_=xn[:, i % NT, :], in_offset=None).then_inc(s_send, 16)
                    pool.wait_ge(s_send, 16 * T)

            s_ld = [sem(f"rows_in{l}_{i}") for i in range(2)]
            s_st = [sem(f"rows_out{l}_{i}") for i in range(2)]
            s_t, s_tc, s_gu, s_ga, s_h = (sem(f"tile_T{l}"), sem(f"tile_Tc{l}"), sem(f"tile_gu{l}"),
                                          sem(f"tile_act{l}"), sem(f"tile_h{l}"))
            s_ht, s_hc, s_dn, s_y = sem(f"tile_hT{l}"), sem(f"tile_hTc{l}"), sem(f"tile_down{l}"), sem(f"tile_y{l}")
            s_first = sem(f"tile_b1{l}")

            with nc.Block() as block:
                @block.sync
                def _(sp):
                    def load(i, par, first=False):
                        at = i * P if first else sp.snap(i * P)
                        if not first:
                            sp.wait_ge(s_t, i - 1)
                        sp.dma_start(rows_in[par], list_x[l][bass.ds(at, P), :]).then_inc(s_ld[par], 16)

                    def store(i, par):
                        at = i * P if isinstance(i, int) else sp.snap(i * P)
                        sp.wait_ge(s_y, i + 1)
                        sp.dma_start(list_y[l][bass.ds(at, P), :], rows_out[par]).then_inc(s_st[par], 16)

                    load(0, 0, True)
                    load(1, 1, True)
                    with sp.Fori(0, NTL // 2) as pair:
                        for par in range(2):
                            load(pair * 2 + par + 2, par)
                            store(pair * 2 + par, par)
                    store(NTL - 1, 0)
                    sp.wait_ge(s_st[0], 16 * (NTL // 2 + 1))
                    sp.wait_ge(s_st[1], 16 * (NTL // 2))
                    for i in range(2):
                        sp.wait_ge(s_ld[i], 16 * (NTL // 2 + 1))

                @block.tensor
                def _(pe):
                    def expert(i):
                        return pe.value_load(tile_e[0:1, bass.ds(i, 1)], min_val=0, max_val=L.experts - 1)

                    def turn_rows(i, par, half):
                        pe.wait_ge(s_ld[par], 16 * (half + 1))
                        for k in range(KD):
                            last = nc.tensor.transpose(ps[:, par, k * P:(k + 1) * P],
                                                       rows_in[par][:, k * P:(k + 1) * P], ident[:, :])
                        last.then_inc(s_t, 1)

                    def up(i, par):
                        e = expert(i)
                        pe.wait_ge(s_tc, i + 1)
                        for n, w in enumerate([w_gate, w_up] if l == 0 else [w_gate]):
                            for k in range(KD):
                                last = nc.tensor.matmul(ps[:, 2 + 2 * par + n, :], rowsT[par][:, k, :],
                                                        w[:, bass.ds(e, 1), k, :].rearrange("p a n -> p (a n)"),
                                                        start=(k == 0), stop=(k == KD - 1))
                        last.then_inc(s_gu, 1)

                    def turn_hidden(i, par):
                        pe.wait_ge(s_h, i + 1)
                        for k in range(4):
                            last = nc.tensor.transpose(ps[:, 6, k * P:(k + 1) * P], hid[par][:, k * P:(k + 1) * P],
                                                       ident[:, :])
                        last.then_inc(s_ht, 1)

                    def down(i, par, first=False):
                        e = expert(i)
                        pe.wait_ge(s_hc, i + 1)
                        if not first:
                            pe.wait_ge(s_y, i)
                        for k in range(4):
                            last = nc.tensor.matmul(ps[:, 7, 0:D], hT[par][:, k, :],
                                                    w_down[:, bass.ds(e, 1), k, :].rearrange("p a n -> p (a n)"),
                                                    start=(k == 0), stop=(k == 3))
                        last.then_inc(s_dn, 1)

                    def step(i, par, half, first=False):
                        turn_rows(i + 1, 1 - par, half + par)
                        turn_hidden(i, par)
                        up(i + 1, 1 - par)
                        down(i, par, first)

                    turn_rows(0, 0, 0)
                    up(0, 0)
                    step(0, 0, 0, True)
                    step(1, 1, 0)
                    with pe.Fori(1, NTL // 2) as pair:
                        step(pair * 2, 0, pair)
                        step(pair * 2 + 1, 1, pair)
                    turn_hidden(NTL - 1, 0)
                    down(NTL - 1, 0)

                @block.scalar
                def _(act):
                    def first_act(i, par):
                        if l == 0:
                            act.wait_ge(s_gu, i + 1)
                            nc.scalar.activation(act_g[par], ps[:, 2 + 2 * par, :], ACT.Silu).then_inc(s_ga, 1)
                        else:
                            act.wait_ge(s_first, i + 1)
                            nc.scalar.activation(hid[par], act_g[par], ACT.Relu).then_inc(s_h, 1)

                    def copy_hT(i, par):
                        act.wait_ge(s_ht, i + 1)
                        nc.scalar.activation(hT[par], ps[:, 6, :].rearrange("p (k n) -> p k n", n=P),
                                             ACT.Copy).then_inc(s_hc, 1)

                    first_act(0, 0)
                    with act.Fori(0, NTL // 2) as pair:
                        for par in range(2):
                            copy_hT(pair * 2 + par, par)
                            first_act(pair * 2 + par + 1, 1 - par)
                    copy_hT(NTL - 1, 0)

                @block.vector
                def _(dve):
                    def copy_rows(i, par):
                        dve.wait_ge(s_t, i + 1)
                        nc.vector.tensor_copy(rowsT[par], ps[:, par, 0:D].rearrange("p (k n) -> p k n", n=P)
                                              ).then_inc(s_tc, 1)

                    def hidden(i, par):
                        if l == 0:
                            dve.wait_ge(s_ga, i + 1)
                            nc.vector.tensor_tensor(hid[par], act_g[par], ps[:, 3 + 2 * par, :], ALU.mult
                                                    ).then_inc(s_h, 1)
                        else:
                            e = dve.value_load(tile_e[0:1, bass.ds(i, 1)], min_val=0, max_val=E - 1)
                            dve.wait_ge(s_gu, i + 1)
                            nc.vector.tensor_tensor(act_g[par], ps[:, 2 + 2 * par, :],
                                                    eb1[:, bass.ds(e, 1), :].rearrange("p a n -> p (a n)"), ALU.add
                                                    ).then_inc(s_first, 1)

                    def finish(i, par, half, first=False):
                        if l == 1:
                            e = dve.value_load(tile_e[0:1, bass.ds(i, 1)], min_val=0, max_val=E - 1)
                        dve.wait_ge(s_dn, i + 1)
                        if not first:
                            dve.wait_ge(s_st[par], 16 * half)
                        if l == 0:
                            nc.vector.tensor_copy(rows_out[par], ps[:, 7, 0:D]).then_inc(s_y, 1)
                        else:
                            nc.vector.tensor_tensor(rows_out[par], ps[:, 7, 0:D],
                                                    eb2[:, bass.ds(e, 1), :].rearrange("p a n -> p (a n)"), ALU.add
                                                    ).then_inc(s_y, 1)

                    copy_rows(0, 0)
                    hidden(0, 0)
                    copy_rows(1, 1)
                    hidden(1, 1)
                    finish(0, 0, 0, True)
                    copy_rows(2, 0)
                    hidden(2, 0)
                    finish(1, 1, 0, True)
                    copy_rows(3, 1)
                    with dve.Fori(1, NTL // 2 - 1) as pair:
                        hidden(pair * 2 + 1, 1)
                        finish(pair * 2, 0, pair)
                        copy_rows(pair * 2 + 2, 0)
                        hidden(pair * 2 + 2, 0)
                        finish(pair * 2 + 1, 1, pair)
                        copy_rows(pair * 2 + 3, 1)
                    n = NTL // 2 - 1
                    hidden(2 * n + 1, 1)
                    finish(2 * n, 0, n)
                    copy_rows(2 * n + 2, 0)
                    hidden(2 * n + 2, 0)
                    finish(2 * n + 1, 1, n)
                    finish(2 * n + 2, 0, n + 1)

            s_back = [sem(f"rows_back{l}_{t}") for t in range(4)]
            s_var2, s_rstd2 = sem(f"back_var{l}"), sem(f"back_rstd{l}")
            s_ysh = [sem(f"shared_back{l}_{b}") for b in range(NB)]
            s_o, s_xf = sem(f"out{l}"), sem(f"x_final{l}")
            with nc.Block() as block:
                @block.gpsimd
                def _(pool):
                    for t in range(NT):
                        for k in range(L.top):
                            i = k * NT + t
                            nc.gpsimd.indirect_dma_start(
                                out=got[k][:, t, :], out_offset=None, in_=list_y[l],
                                in_offset=bass.IndirectOffsetOnAxis(ap=slot[:, i:i + 1], axis=0)
                            ).then_inc(s_back[t // TB], 16)

                if l == 1:
                    @block.scalar
                    def _(act):
                        for b in range(NB):
                            take_root(act, range(b * TB, (b + 1) * TB), s_var2, s_rstd2, b + 1)

                @block.sync
                def _(sp):
                    if l == 0:
                        for b in range(NB):
                            sp.dma_start(got[1][:, b * TB:(b + 1) * TB, :],
                                         list_y[0][b * QB:(b + 1) * QB, :].rearrange("(t p) d -> p t d", p=P)
                                         ).then_inc(s_ysh[b], 16)
                    else:
                        dst = out.rearrange("o (t p) d -> p (o t) d", p=P)
                        for b in range(NB):
                            sp.wait_ge(s_xf, b + 1)
                            sp.dma_start(dst[:, b * TB:(b + 1) * TB, :], x[:, b * TB:(b + 1) * TB, :]).then_inc(s_o, 16)
                        sp.wait_ge(s_o, 16 * NB)

                @block.vector
                def _(dve):
                    tg = tgate[:, 2 + l:3 + l]
                    chain = Chain(dve, f"back_chain{l}")
                    if l == 1:
                        nc.vector.tensor_scalar(gamma[:, :], gamma[:, :], tg, None, ALU.mult)
                        chain(nc.vector.tensor_scalar(beta[:, :], beta[:, :], tg, None, ALU.mult))
                    for b in range(NB):
                        ts = slice(b * TB, (b + 1) * TB)
                        dve.wait_ge(s_back[b], 16 * TB * L.top)
                        if l == 0:
                            dve.wait_ge(s_ysh[b], 16)
                            chain(nc.vector.tensor_tensor(got[0][:, ts, :], got[0][:, ts, :], got[1][:, ts, :], ALU.add))
                            chain(nc.vector.scalar_tensor_tensor(
                                out=x[:, ts, :].rearrange("p t d -> p (t d)"),
                                in0=got[0][:, ts, :].rearrange("p t d -> p (t d)"), scalar=tg,
                                in1=x[:, ts, :].rearrange("p t d -> p (t d)"), op0=ALU.mult, op1=ALU.add))
                            continue
                        for t in range(b * TB, (b + 1) * TB):
                            last = nc.vector.scalar_tensor_tensor(out=xn[:, t, :], in0=got[0][:, t, :],
                                                                  scalar=wts[:, 2, t:t + 1], in1=xn[:, t, :],
                                                                  op0=ALU.mult, op1=ALU.add)
                        chain(last)
                        for t in range(b * TB, (b + 1) * TB):
                            last = nc.vector.scalar_tensor_tensor(out=got[0][:, t, :], in0=got[1][:, t, :],
                                                                  scalar=wts[:, 1, t:t + 1], in1=xn[:, t, :],
                                                                  op0=ALU.mult, op1=ALU.add)
                        chain(last)
                        layer_norm_stats(dve, chain, got[0], range(b * TB, (b + 1) * TB), s_var2, s_rstd2, b + 1)
                        for t in range(b * TB, (b + 1) * TB):
                            last = normalize(got[0], got[0], t)
                        chain(last)
                        gb = gamma[:, :].unsqueeze(1).broadcast_to([P, TB, D])
                        bb = beta[:, :].unsqueeze(1).broadcast_to([P, TB, D])
                        chain(nc.vector.tensor_tensor(got[0][:, ts, :], got[0][:, ts, :], gb, ALU.mult))
                        chain(nc.vector.tensor_tensor(x[:, ts, :], x[:, ts, :], bb, ALU.add))
                        nc.vector.tensor_tensor(x[:, ts, :], x[:, ts, :], got[0][:, ts, :], ALU.add).then_inc(s_xf, 1)

        def dump():
            s_o = sem("dump")
            with nc.Block() as block:
                @block.sync
                def _(sp):
                    sp.dma_start(out.rearrange("o (t p) d -> p (o t) d", p=P), x[:, :, :]).then_inc(s_o, 16)
                    sp.wait_ge(s_o, 16)

        n = 0
        for L in layers:
            attention(L)
            free_semaphores()
            n += 1
            if n == stage:
                return dump()
            moe(L)
            free_semaphores()
            n += 1
            if n == stage and n < 4:
                return dump()


def layout(inputs, np):
    t = {k: np.asarray(v) for k, v in inputs.items()}
    kv = t["L0_xattn_Wkv"].reshape(H, 2, DH, C)
    bkv = t["L0_xattn_bkv"].reshape(H, 2, DH)
    swap = lambda w: np.ascontiguousarray(np.swapaxes(w, -1, -2))
    flat = np.ascontiguousarray
    col = lambda b: flat(b.reshape(-1, P).T)
    return {
        "x": flat(t["x"]), "ctxT": swap(t["ctx_768"][0]), "g_xattn": t["g_xattn"], "g_ffn": t["g_ffn"],
        "wq0": swap(t["L0_xattn_Wq"]), "bq0": col(t["L0_xattn_bq"]),
        "wk0": swap(kv[:, 0].reshape(D, C)), "wv0": swap(kv[:, 1].reshape(D, C)),
        "bk0": col(flat(bkv[:, 0])), "bv0": flat(bkv[:, 1]).reshape(D),
        "wo": swap(t["L0_xattn_Wo"]), "bo0": t["L0_xattn_bo"],
        "rw0": swap(t["L0_ffn_gate_w"]),
        "sg": swap(t["L0_ffn_shared_gate"]), "su": swap(t["L0_ffn_shared_up"]), "sd": swap(t["L0_ffn_shared_down"]),
        "rg": swap(t["L0_ffn_r_gate"]), "ru": swap(t["L0_ffn_r_up"]), "rd": swap(t["L0_ffn_r_down"]),
        "wq1": t["L1_xattn_Wq"], "bq1": col(t["L1_xattn_bq"]), "wk1": t["L1_xattn_Wk"], "bk1": col(t["L1_xattn_bk"]),
        "wv1": t["L1_xattn_Wv"], "bv1": t["L1_xattn_bv"], "w1": t["L1_xattn_W1"], "b1": col(t["L1_xattn_b1"]),
        "w2": t["L1_xattn_W2"], "bo1": t["L1_xattn_b2"],
        "rw1": t["L1_ffn_Wg"], "rb1": t["L1_ffn_bg"], "ew1": t["L1_ffn_W1"], "eb1": t["L1_ffn_b1"],
        "ew2": t["L1_ffn_W2"], "eb2": t["L1_ffn_b2"], "gamma": t["L1_ffn_gamma"], "beta": t["L1_ffn_beta"],
    }


def kernel(**inputs):
    import numpy as np
    import concourse.bacc as bacc
    from concourse.bass_utils import run_bass_kernel_spmd

    nc = bacc.Bacc("TRN2", target_bir_lowering=False, num_devices=1)
    arrays = {f"in_{k}": v for k, v in layout(inputs, np).items()}
    aps = {k[3:]: nc.dram_tensor(k, v.shape, mybir.dt.from_np(v.dtype), kind="ExternalInput").ap()
           for k, v in arrays.items()}
    out = nc.dram_tensor("out_x", (1, S, D), F32, kind="ExternalOutput").ap()
    build(nc, aps, out)
    r = run_bass_kernel_spmd(nc, [arrays], core_ids=[0])
    return r.results[0]["out_x"]
```

```python
from contextlib import ExitStack

import concourse.bass as bass
from concourse import mybir

F32 = mybir.dt.float32
BF16 = mybir.dt.bfloat16
I32 = mybir.dt.int32
U32 = mybir.dt.uint32
ALU = mybir.AluOpType
ACT = mybir.ActivationFunctionType
AX = mybir.AxisListType

P = 128
S, D = 2048, 256
M, C = 1601, 192
H, DH = 16, 16
F, E = 512, 8
EPS = 1e-5
SCALE = 1.0 / DH ** 0.5

NT = S // P
KD = D // P
NC = -(-M // P)
MP = NC * P
CH = C // 2
QB = 512
NB = S // QB
TB = QB // P
HG = 4
NG = H // HG
KB = MP // 4
KLAST = M - 3 * KB
VW = 32
ROWS = 6 * DH
SHIFT = 3
STEPS = NG * NC * 2
SB = 3
KC = KB // 4
MW = (M - 1) // 4 + 1
SAFE = 40.0
QPART = [0, 0, 1, 1, 0, 2]
KPART = [0, 1, 0, 1, 2, 0]


class Layer:

    def __init__(self, n):
        self.n = n
        self.mlp = n == 1
        self.top = n + 1
        self.shared = NT if n == 0 else 0
        self.slots = self.top * NT
        self.tiles = self.shared + self.slots + E - 1
        self.tiles += 1 - self.tiles % 2
        self.experts = E + (n == 0)


def build(nc, a, out, stage=99):
    ctx = ExitStack()
    with ctx:
        def sb(name, shape, dt=F32):
            return ctx.enter_context(nc.sbuf_tensor(name, shape, dt))

        layers = [Layer(0), Layer(1)]
        parts_dram = {
            "k": [nc.dram_tensor(f"k_parts{l}", [3, D, MP], BF16).ap() for l in range(2)],
            "q": [nc.dram_tensor(f"q_parts{l}", [3, D, S], BF16).ap() for l in range(2)],
        }
        shift_dram = [nc.dram_tensor(f"shift{l}", [SHIFT, H, S], BF16).ap() for l in range(2)]
        list_x = [nc.dram_tensor(f"list_x{l.n}", [(l.tiles + 1) * P, D], F32).ap() for l in layers]
        list_y = [nc.dram_tensor(f"list_y{l.n}", [l.tiles * P, D], F32).ap() for l in layers]

        x = sb("x", [P, NT, D])
        xn = sb("xn", [P, NT, D])
        zero = sb("zero", [P, D])
        ctxT = sb("ctxT", [CH, 2, MP])
        ident = sb("ident", [P, P])
        below = sb("below", [P, P])
        ones = sb("ones", [P, P])
        head_rows = sb("head_rows", [P, 8], BF16)
        norms = sb("norms", [P, 8])
        top2 = sb("top2", [P, 2, 2])
        unsafe = sb("unsafe", [P, 1], I32)
        valid = sb("valid", [P, 1])
        iota8 = sb("iota8", [P, E])
        iota_tile = sb("iota_tile", [P, 48])
        gates = sb("gates", [P, 4])
        tgate = sb("tgate", [P, 4])
        wq = sb("wq", [P, KD, D])
        wk = sb("wk", [CH, 2, D])
        wv = sb("wv", [CH, 2, D])
        bq = sb("bq", [P, KD])
        bqs = sb("bqs", [P, KD])
        bk = sb("bk", [P, KD])
        bv = sb("bv", [P, D])
        w1 = sb("w1", [P, KD, 2 * D])
        b1 = sb("b1", [P, 4])
        w2 = sb("w2", [P, 4, D])
        b2 = sb("b2", [P, 2, D])
        rw = sb("rw", [P, KD, E])
        rb = sb("rb", [P, E])
        stats = sb("stats", [P, TB, 6])
        mv = sb("mv", [P, TB, 2])
        var_e = sb("var_e", [P, TB])
        var_h = sb("var_h", [P, TB])
        half_bits = sb("half_bits", [P, TB], I32)
        root_bits = sb("root_bits", [P, TB], I32)
        rstd = root_bits[:, :].bitcast(F32)
        newton = sb("newton", [P, TB])

        arena = sb("arena", [P, 28160])
        work = sb("work", [P, 5632])

        def view(region, at, shape, dt=F32):
            n = 1
            for s in shape:
                n *= s
            words = n if dt != BF16 else n // 2
            v = region[:, at:at + words]
            if dt != F32:
                v = v.bitcast(dt)
            if len(shape) == 2:
                v = v.rearrange("p (a b) -> p a b", b=shape[1])
            elif len(shape) == 3:
                v = v.rearrange("p (a b c) -> p a b c", b=shape[1], c=shape[2])
            return v, at + words

        k2, at = view(arena, 0, [H, MP], BF16)
        v_aug, at = view(arena, at, [NC, H, VW])
        q2, at = view(arena, at, [H, QB], BF16)
        probs, _ = view(arena, at, [2, HG, QB])
        xnT = [None, None]
        full = [None, None]
        for i in range(2):
            xnT[i], at = view(arena, at, [KD, QB])
            full[i], at = view(arena, at, [KD, QB])
        part = [[None] * 3, [None] * 3]
        at = 0
        for i in range(2):
            for j in range(3):
                part[i][j], at = view(work, at, [KD, QB], BF16)
        rest, at = view(work, at, [KD, QB])
        squares, at = view(work, at, [2, KD, QB], BF16)
        at = 0
        top_neg = work[:, 0:NT]
        max_full = work[0:NT, NT:NT + P]
        max_rest = work[0:NT, NT + P:NT + 2 * P]
        max_parts = [work[0:NT, NT + (4 + i) * P // 2:NT + (5 + i) * P // 2].bitcast(BF16) for i in range(SHIFT)]
        pv_sb, at = view(work, at, [QB])
        sums, at = view(work, at, [QB])
        o_norm, at = view(work, at, [2, QB])
        oT, at = view(work, at, [KD, QB])
        hidT, at = view(work, at, [4, QB])
        y_tmp, at = view(work, at, [2 * D])
        w_gate, at = view(arena, 0, [E + 1, KD, F])
        w_up, at = view(arena, at, [E + 1, KD, F])
        w_down, at = view(arena, at, [E + 1, 4, D])
        eb1, at1 = view(arena, (E + 1) * KD * F, [E, F])
        eb2, at1 = view(arena, at1, [E, D])
        got = [view(arena, i * NT * D, [NT, D])[0] for i in range(2)]
        at = 0
        rows_in = [None] * 2
        rowsT = [None] * 2
        act_g = [None] * 2
        hid = [None] * 2
        hT = [None] * 2
        rows_out = [None] * 2
        for i in range(2):
            rows_in[i], at = view(work, at, [D])
            rowsT[i], at = view(work, at, [KD, P])
            act_g[i], at = view(work, at, [F])
            hid[i], at = view(work, at, [F])
            hT[i], at = view(work, at, [4, P])
            rows_out[i], at = view(work, at, [D])
        TS = 2 * NT
        lg = sb("lg", [P, NT, E])
        mx = sb("mx", [P, NT, 8])
        ix = sb("ix", [P, NT, 8], U32)
        ixf = sb("ixf", [P, NT, 8])
        wts = sb("wts", [P, 3, NT])
        oh = sb("oh", [P, TS, E])
        tot = sb("tot", [P, TS, E])
        scan = [sb(f"scan{i}", [P, TS, E]) for i in range(2)]
        ends = [sb(f"ends{i}", [P, E]) for i in range(2)]
        padc = sb("padc", [P, 2, E])
        padi = sb("padi", [P, 2, E], I32)
        slotf = sb("slotf", [P, TS])
        slot = sb("slot", [P, TS], U32)
        tilef = sb("tilef", [P, 48])
        tile_e = sb("tile_e", [P, 48], I32)
        gamma = sb("gamma", [P, D])
        beta = sb("beta", [P, D])

        ps = ctx.enter_context(nc.psum_tensor("ps", [P, 8, 512], F32))

        sems = {}

        def sem(name):
            if name not in sems:
                sems[name] = nc.alloc_semaphore(name)
            return sems[name]

        def free_semaphores():
            nc.clear_and_free_semaphores(list(sems.values()))
            nc.all_engine_barrier()
            sems.clear()

        class Chain:

            def __init__(self, eng, name):
                self.eng, self.sem, self.n = eng, sem(name), 0

            def __call__(self, ins):
                self.n += 1
                ins.then_inc(self.sem, 1)
                self.eng.wait_ge(self.sem, self.n)

        def spread(ap, n):
            return ap.rearrange("(a n) -> a n", a=1).broadcast_to([P, n])

        s_x, s_ctx = [sem(f"x_in{b}") for b in range(NB)], sem("ctx_in")
        with nc.Block() as block:
            s_zero, s_set, s_gate, s_sz = sem("zero_set"), sem("consts_set"), sem("gates_in"), sem("shift_zeroed")

            @block.sync
            def _(sp):
                src = a["x"].rearrange("o (t p) d -> p (o t) d", p=P)
                for i, (name, l) in enumerate([("g_xattn", 0), ("g_ffn", 0)]):
                    sp.dma_start(gates[:, 2 * i:2 * i + 2], spread(a[name], 2)).then_inc(s_gate, 16)
                for k in range(2):
                    sp.dma_start(ctxT[:, k, 0:M], a["ctxT"][k * CH:(k + 1) * CH, :]).then_inc(s_ctx, 16)
                for b in range(NB):
                    sp.dma_start(x[:, b * TB:(b + 1) * TB, :], src[:, b * TB:(b + 1) * TB, :]).then_inc(s_x[b], 16)
                sp.wait_ge(s_zero, 1)
                for l in range(2):
                    sp.dma_start(shift_dram[l].rearrange("r h s -> (r h) s").rearrange("a (n s) -> a n s", n=4),
                                 zero[0:SHIFT * H, :].bitcast(BF16).unsqueeze(1).broadcast_to([SHIFT * H, 4, 2 * D])
                                 ).then_inc(s_sz, 16)

            @block.vector
            def _(dve):
                nc.vector.memset(zero[:, :], 0.0).then_inc(s_zero, 1)
                nc.vector.memset(ctxT[:, :, M:MP], 0.0)
                nc.vector.memset(ones[:, :], 1.0).then_inc(s_set, 1)

            @block.scalar
            def _(act):
                act.wait_ge(s_gate, 32)
                nc.scalar.activation(tgate[:, :], gates[:, :], ACT.Tanh)

            @block.gpsimd
            def _(pool):
                chain = Chain(pool, "const_chain")
                chain(nc.gpsimd.memset(ident[:, :], 0.0))
                nc.gpsimd.affine_select(out=ident[:, :], in_=ident[:, :], compare_op=ALU.not_equal, fill=1.0,
                                        base=0, pattern=[[-1, P]], channel_multiplier=1)
                chain(nc.gpsimd.memset(below[:, :], 0.0))
                nc.gpsimd.affine_select(out=below[:, :], in_=below[:, :], compare_op=ALU.is_ge, fill=1.0,
                                        base=0, pattern=[[-1, P]], channel_multiplier=1)
                chain(nc.gpsimd.memset(head_rows[:, :], 1.0))
                chain(nc.gpsimd.affine_select(out=head_rows[:, :], in_=head_rows[:, :], compare_op=ALU.is_ge, fill=0.0,
                                              base=0, pattern=[[-DH, 8]], channel_multiplier=1))
                nc.gpsimd.affine_select(out=head_rows[:, :], in_=head_rows[:, :], compare_op=ALU.is_ge, fill=0.0,
                                        base=DH - 1, pattern=[[DH, 8]], channel_multiplier=-1)
                chain(nc.gpsimd.memset(valid[:, :], 0.0))
                nc.gpsimd.affine_select(out=valid[:, :], in_=valid[:, :], compare_op=ALU.is_ge, fill=1.0,
                                        base=-(M - (NC - 1) * P), pattern=[[0, 1]], channel_multiplier=1)
                nc.gpsimd.iota(iota8[:, :], pattern=[[1, E]], base=0, channel_multiplier=0,
                               allow_small_or_imprecise_dtypes=True)
                nc.gpsimd.iota(iota_tile[:, :], pattern=[[P, 48]], base=0, channel_multiplier=0,
                               allow_small_or_imprecise_dtypes=True)

        def norm_rows(step, src, dst):
            for t in range(TB):
                last = nc.vector.bn_stats(stats[:, t, :], src(t))
            step(last)
            for t in range(TB):
                last = nc.vector.bn_aggr(mv[:, t, :], stats[:, t, :])
            step(last)
            step(nc.vector.tensor_scalar(var_e[:, :], mv[:, :, 1], EPS, None, ALU.add))
            nc.vector.tensor_scalar(var_h[:, :], var_e[:, :], -0.5, None, ALU.mult)
            step(nc.vector.tensor_scalar(half_bits[:, :], var_e[:, :].bitcast(I32), 1, None,
                                         ALU.logical_shift_right))
            step(nc.vector.tensor_scalar(root_bits[:, :], half_bits[:, :], -1.0, float(0x5F3759DF), ALU.mult, ALU.add))
            for _ in range(4):
                step(nc.vector.tensor_tensor(newton[:, :], rstd, rstd, ALU.mult))
                step(nc.vector.tensor_tensor(newton[:, :], newton[:, :], var_h[:, :], ALU.mult))
                step(nc.vector.scalar_tensor_tensor(out=rstd, in0=newton[:, :], scalar=1.5, in1=rstd, op0=ALU.add,
                                                    op1=ALU.mult))
            for t in range(TB):
                last = nc.vector.tensor_scalar(dst(t), src(t), mv[:, t, 0:1], rstd[:, t:t + 1], ALU.subtract,
                                               ALU.mult)
            return last

        def attention(L):
            l = L.n
            s_w, s_kv, s_xn = sem(f"attn_weights{l}"), sem(f"kv_weights{l}"), sem(f"xn{l}")
            s_xt, s_xtc = sem(f"xn_transposed{l}"), sem(f"xnT_copied{l}")
            s_pr, s_hi, s_sp = sem(f"projected{l}"), sem(f"high_parts{l}"), sem(f"split{l}")
            s_po = [sem(f"parts_stored{l}_{i}") for i in range(2)]
            s_v, s_va = sem(f"v_projected{l}"), sem(f"v_copied{l}")
            s_vz, s_ko, s_bqs, s_full = sem(f"v_zeroed{l}"), sem(f"k_ones{l}"), sem(f"bq_scaled{l}"), sem(f"full{l}")
            s_sq, s_nrm, s_nmx, s_top, s_all, s_uns, s_nz = (
                sem(f"squared{l}"), sem(f"norm_sums{l}"), sem(f"norm_maxima{l}"), sem(f"norm_top{l}"),
                sem(f"norm_all{l}"), sem(f"unsafe{l}"), sem(f"norms_zeroed{l}"))
            s_k2, s_q2 = sem(f"k2_in{l}"), [sem(f"q2_in{l}_{g}") for g in range(NG)]
            items = [("k", n) for n in range(4)] + [("q", b) for b in range(NB)]

            def load_q2(eng, at, g, done=None):
                cols = bass.ds(at, QB)
                for i, j in enumerate(QPART):
                    eng.dma_start(q2[i * DH:(i + 1) * DH, HG * g:HG * g + HG, :],
                                  parts_dram["q"][l][j, :, cols].rearrange("(h d) s -> d h s", d=DH)
                                  [:, HG * g:HG * g + HG, :]).then_inc(done or s_q2[g], 16)
                eng.dma_start(q2[ROWS:ROWS + SHIFT, HG * g:HG * g + HG, :],
                              shift_dram[l][:, HG * g:HG * g + HG, cols]).then_inc(done or s_q2[g], 16)

            with nc.Block() as block:
                @block.sync
                def _(sp):
                    for k in range(2):
                        sp.dma_start(wk[:, k, :], a[f"wk{l}"][k * CH:(k + 1) * CH, :]).then_inc(s_kv, 16)
                        sp.dma_start(wv[:, k, :], a[f"wv{l}"][k * CH:(k + 1) * CH, :]).then_inc(s_kv, 16)
                    sp.dma_start(bk[:, :], a[f"bk{l}"]).then_inc(s_kv, 16)
                    sp.dma_start(bv[:, :], spread(a[f"bv{l}"], D)).then_inc(s_kv, 16)
                    sp.dma_start(wq[:, :, :], a[f"wq{l}"].rearrange("(k p) n -> p k n", p=P)).then_inc(s_kv, 16)
                    sp.dma_start(bq[:, :], a[f"bq{l}"]).then_inc(s_kv, 16)
                    if L.mlp:
                        sp.dma_start(w1[:, :, :], a["w1"].rearrange("(k p) n -> p k n", p=P)).then_inc(s_w, 16)
                        sp.dma_start(b1[:, :], a["b1"]).then_inc(s_w, 16)
                        sp.dma_start(w2[:, :, :], a["w2"].rearrange("(k p) n -> p k n", p=P)).then_inc(s_w, 16)
                    else:
                        sp.dma_start(w2[:, 0:KD, :], a["wo"].rearrange("(k p) n -> p k n", p=P)).then_inc(s_w, 16)
                    for i in range(2):
                        sp.dma_start(b2[:, i, :], spread(a[f"bo{l}"], D)).then_inc(s_w, 16)
                    sp.wait_ge(s_ko, 1)
                    sp.dma_start(k2[ROWS:ROWS + SHIFT, 1:H, :],
                                 k2[ROWS:ROWS + SHIFT, 0:1, :].broadcast_to([SHIFT, H - 1, MP])).then_inc(s_k2, 16)
                    for n, (kind, b) in enumerate(items):
                        w = KB if kind == "k" else QB
                        sp.wait_ge(s_sp, n + 1)
                        for j in range(3):
                            sp.dma_start(parts_dram[kind][l][j, :, b * w:(b + 1) * w]
                                         .rearrange("(k p) s -> p k s", p=P),
                                         part[n % 2][j][:, :, 0:w]).then_inc(s_po[n % 2], 16)
                        if n == 3:
                            for i in range(2):
                                sp.wait_ge(s_po[i], 96)
                            for i, j in enumerate(KPART):
                                sp.dma_start(k2[i * DH:(i + 1) * DH, :, :],
                                             parts_dram["k"][l][j].rearrange("(h d) s -> d h s", d=DH)
                                             ).then_inc(s_k2, 16)
                        if n == 5:
                            sp.wait_ge(s_po[0], 144)
                            if l == 0:
                                sp.wait_ge(s_sz, 32)
                            for g in range(NG):
                                load_q2(sp, 0, g)
                    sp.wait_ge(s_k2, 112)
                    for g in range(NG):
                        sp.wait_ge(s_q2[g], 16 * 7)
                    sp.wait_ge(s_po[0], 192)
                    sp.wait_ge(s_po[1], 192)
                    sp.wait_ge(s_w, 16 * (5 if L.mlp else 3))

                @block.scalar
                def _(act):
                    act.wait_ge(s_kv, 128)
                    nc.scalar.activation(bqs[:, :], bq[:, :], ACT.Copy, scale=SCALE).then_inc(s_bqs, 1)
                    act.wait_ge(s_bqs, 1)
                    for n, (kind, b) in enumerate(items):
                        w = KB if kind == "k" else QB
                        if kind == "k" and b == 3:
                            w = KLAST
                        if kind == "q":
                            act.wait_ge(s_xt, b + 1)
                            nc.scalar.activation(xnT[b % 2], ps[:, 2 * (b % 2):2 * (b % 2) + 2, :],
                                                 ACT.Copy).then_inc(s_xtc, 1)
                        bank = 4 + 2 * (n % 2)
                        bias = bk if kind == "k" else bqs
                        scale = 1.0 if kind == "k" else SCALE
                        act.wait_ge(s_pr, n + 1)
                        if n >= 2:
                            act.wait_ge(s_sp, n - 1)
                            act.wait_ge(s_sq, n - 1)
                            act.wait_ge(s_po[n % 2], 48 * (n // 2))
                        for k in range(KD):
                            nc.scalar.activation(full[n % 2][:, k, 0:w], ps[:, bank + k, 0:w], ACT.Identity,
                                                 bias=bias[:, k:k + 1], scale=scale).then_inc(s_full, 1)
                            last = nc.scalar.activation(part[n % 2][0][:, k, 0:w], ps[:, bank + k, 0:w],
                                                        ACT.Identity, bias=bias[:, k:k + 1], scale=scale)
                            last.then_inc(s_hi, 1)

                @block.tensor
                def _(pe):
                    pe.wait_ge(s_kv, 128)
                    if l == 0:
                        pe.wait_ge(s_ctx, 32)

                    def transpose_block(b):
                        pe.wait_ge(s_xn, b + 1)
                        for t in range(TB):
                            for k in range(KD):
                                last = nc.tensor.transpose(ps[:, 2 * (b % 2) + k, t * P:(t + 1) * P],
                                                           xn[:, b * TB + t, k * P:(k + 1) * P], ident[:, :])
                        last.then_inc(s_xt, 1)

                    def norm(n):
                        pe.wait_ge(s_sq, n + 1)
                        c = KC if items[n][0] == "k" else P
                        for t in range(4):
                            for k in range(KD):
                                at = (t * KD + k) * 8
                                last = nc.tensor.matmul(ps[0:c, 4 + 2 * (n % 2), at:at + 8],
                                                        squares[:, n % 2, k, t * c:(t + 1) * c], head_rows[:, :],
                                                        start=True, stop=True)
                        last.then_inc(s_nrm, 1)

                    for n, (kind, b) in enumerate(items):
                        bank = 4 + 2 * (n % 2)
                        if n == 3:
                            transpose_block(0)
                        if kind == "q" and b + 1 < NB:
                            if b >= 1:
                                pe.wait_ge(s_xtc, b)
                            transpose_block(b + 1)
                        if kind == "q":
                            pe.wait_ge(s_xtc, b + 1)
                        if n >= 2:
                            pe.wait_ge(s_nmx, n - 1)
                        for ko in range(KD):
                            for ki in range(2):
                                if kind == "k":
                                    w = KB if b < 3 else KLAST
                                    last = nc.tensor.matmul(ps[:, bank + ko, 0:w], wk[:, ki, ko * P:(ko + 1) * P],
                                                            ctxT[:, ki, b * KB:b * KB + w],
                                                            start=(ki == 0), stop=(ki == 1))
                                else:
                                    last = nc.tensor.matmul(ps[:, bank + ko, :], wq[:, ki, ko * P:(ko + 1) * P],
                                                            xnT[b % 2][:, ki, :], start=(ki == 0), stop=(ki == 1))
                        last.then_inc(s_pr, 1)
                        if n >= 1:
                            norm(n - 1)
                    norm(len(items) - 1)
                    for c in range(NC):
                        bank = c % 4
                        if c == 0:
                            pe.wait_ge(s_xtc, NB)
                        if c >= 4:
                            pe.wait_ge(s_va, c - 3)
                        for ki in range(2):
                            last = nc.tensor.matmul(ps[:, bank, 0:D], ctxT[:, ki, c * P:(c + 1) * P], wv[:, ki, :],
                                                    start=(ki == 0), stop=(ki == 1))
                        last.then_inc(s_v, 1)

                @block.vector
                def _(dve):
                    chain = Chain(dve, f"prep_chain{l}")

                    def norm_block(b):
                        if l == 0:
                            dve.wait_ge(s_x[b], 16)
                        norm_rows(chain, lambda t: x[:, b * TB + t, :], lambda t: xn[:, b * TB + t, :]
                                  ).then_inc(s_xn, 1)

                    chain(nc.vector.memset(norms[:, :], 0.0))
                    norm_block(0)
                    for n, (kind, b) in enumerate(items):
                        w = KB if kind == "k" else QB
                        i = n % 2
                        if kind == "k" and b == 3:
                            w = KLAST
                        dve.wait_ge(s_hi, KD * (n + 1))
                        chain(nc.vector.tensor_tensor(rest[:, :, 0:w], full[i][:, :, 0:w], part[i][0][:, :, 0:w],
                                                      ALU.subtract))
                        chain(nc.vector.tensor_copy(part[i][1][:, :, 0:w], rest[:, :, 0:w]))
                        if w == KLAST:
                            for j in range(3):
                                chain(nc.vector.memset(part[i][j][:, :, w:KB], 0.0))
                        nc.vector.tensor_tensor(part[i][2][:, :, 0:w], rest[:, :, 0:w], part[i][1][:, :, 0:w],
                                                ALU.subtract).then_inc(s_sp, 1)
                        dve.wait_ge(s_sp, n + 1)
                        if n + 1 < NB:
                            norm_block(n + 1)
                        dve.wait_ge(s_nrm, n + 1)
                        c = KC if kind == "k" else P
                        nc.vector.tensor_reduce(norms[0:c, n:n + 1], ps[0:c, 4 + 2 * i, 0:8 * 8], AX.X, ALU.max
                                                ).then_inc(s_nmx, 1)
                    dve.wait_ge(s_nmx, len(items))
                    nc.vector.tensor_reduce(top2[:, 0, :], norms[:, :].rearrange("p (a b) -> p a b", a=2), AX.X,
                                            ALU.max).then_inc(s_top, 1)
                    for c in range(NC):
                        if c == 0:
                            dve.wait_ge(s_vz, 1)
                        dve.wait_ge(s_v, c + 1)
                        last = nc.vector.tensor_tensor(
                            v_aug[:, c, :, 0:DH], ps[:, c % 4, 0:D].rearrange("p (h d) -> p h d", d=DH),
                            bv[:, :].rearrange("p (h d) -> p h d", d=DH), ALU.add)
                        last.then_inc(s_va, 1)
                    dve.wait_ge(s_va, NC)
                    chain(nc.vector.tensor_scalar(v_aug[:, NC - 1, :, :], v_aug[:, NC - 1, :, :],
                                                  valid[:, 0:1], None, ALU.mult))
                    dve.wait_ge(s_all, 1)
                    chain(nc.vector.tensor_tensor(top2[:, 0, 0:1], top2[:, 1, 0:1], top2[:, 1, 1:2], ALU.mult))
                    chain(nc.vector.tensor_scalar(unsafe[:, :], top2[:, 0, 0:1], SAFE * SAFE, None, ALU.is_gt))

                @block.gpsimd
                def _(pool):
                    chain = Chain(pool, f"fill_chain{l}")
                    chain(nc.gpsimd.memset(k2[ROWS:ROWS + SHIFT, 0, M:MP], 0.0))
                    nc.gpsimd.memset(k2[ROWS:ROWS + SHIFT, 0, 0:M], 1.0).then_inc(s_ko, 1)
                    pool.wait_ge(s_ko, 1)
                    chain(nc.gpsimd.memset(v_aug, 0.0))
                    nc.gpsimd.memset(v_aug[:, :, :, DH:DH + 1], 1.0).then_inc(s_vz, 1)
                    pool.wait_ge(s_vz, 1)
                    for n, (kind, b) in enumerate(items):
                        i, w = n % 2, KB if kind == "k" else QB
                        if n == 3:
                            w = KLAST
                            pool.wait_ge(s_nrm, n - 1)
                            chain(nc.gpsimd.memset(squares[:, i, :, KLAST:KB], 0.0))
                        elif n >= 2:
                            pool.wait_ge(s_nrm, n - 1)
                        pool.wait_ge(s_full, KD * (n + 1))
                        nc.gpsimd.tensor_tensor(squares[:, i, :, 0:w], full[i][:, :, 0:w], full[i][:, :, 0:w],
                                                ALU.mult).then_inc(s_sq, 1)
                    pool.wait_ge(s_top, 1)
                    nc.gpsimd.partition_all_reduce(top2[:, 1, :], top2[:, 0, :], P, bass.bass_isa.ReduceOp.max
                                                   ).then_inc(s_all, 1)

            s_hq, s_ms, s_mm, s_mt, s_mc, s_mo, s_md = (
                sem(f"head_q{l}"), sem(f"max_scores{l}"), sem(f"max_taken{l}"), sem(f"max_turned{l}"),
                sem(f"max_copied{l}"), sem(f"max_split{l}"), sem(f"shift_stored{l}"))
            s_m1, s_m2, s_m3 = [sem(f"max_part{l}_{i}") for i in range(3)]
            s_re = sem(f"q2_again{l}")
            q_head = q2.rearrange("p h s -> p (h s)")[:, 0:S]
            with nc.Block() as block:
                def asked(eng):
                    return eng.If(eng.value_load(unsafe[0:1, 0:1], min_val=0, max_val=1) > 0)

                @block.sync
                def _(sp):
                    with asked(sp):
                        def load_head(h):
                            for i, j in enumerate(QPART):
                                sp.dma_start(q_head[i * DH:(i + 1) * DH, :],
                                             parts_dram["q"][l][j].rearrange("(h d) s -> h d s", d=DH)
                                             [bass.ds(h, 1), :, :].rearrange("a d s -> (a d) s")
                                             ).then_inc(s_hq, 16)

                        def store_head(h):
                            sp.wait_ge(s_mo, h + 1)
                            for j in range(SHIFT):
                                sp.dma_start(shift_dram[l][j, bass.ds(h, 1), :]
                                             .rearrange("a (t q) -> (a t) q", q=P), max_parts[j]).then_inc(s_md, 16)

                        load_head(0)
                        store_head(0)
                        with sp.Fori(1, H) as h:
                            load_head(h)
                            store_head(h)
                        sp.wait_ge(s_md, 16 * SHIFT * H)
                        for g in range(NG):
                            load_q2(sp, 0, g, s_re)
                        sp.wait_ge(s_re, 16 * 7 * NG)

                @block.tensor
                def _(pe):
                    with asked(pe):
                        def head(h, first):
                            pe.wait_ge(s_hq, 96 if first else h * 96 + 96)
                            for t in range(NT):
                                bank = 4 * (t % 2)
                                if t >= 2:
                                    pe.wait_ge(s_mm, t - 1 if first else h * NT + t - 1)
                                for i in range(4):
                                    last = nc.tensor.matmul(
                                        ps[:, bank + i, 0:MW], q_head[0:ROWS, t * P:(t + 1) * P],
                                        k2[0:ROWS, bass.ds(h, 1), i * (MW - 1):i * (MW - 1) + MW]
                                        .rearrange("p a n -> p (a n)"), start=True, stop=True)
                                last.then_inc(s_ms, 1)
                            pe.wait_ge(s_mm, NT if first else h * NT + NT)
                            nc.tensor.transpose(ps[0:NT, 0, 0:P], top_neg, ident[:, :]).then_inc(s_mt, 1)
                            pe.wait_ge(s_mc, 1 if first else h + 1)
                        head(0, True)
                        with pe.Fori(1, H) as h:
                            head(h, False)

                @block.vector
                def _(dve):
                    with asked(dve):
                        def head(h, first):
                            for t in range(NT):
                                dve.wait_ge(s_ms, t + 1 if first else h * NT + t + 1)
                                nc.vector.tensor_reduce(top_neg[:, t:t + 1], ps[:, 4 * (t % 2):4 * (t % 2) + 4, 0:MW],
                                                        AX.XY, ALU.max, negate=True).then_inc(s_mm, 1)
                            dve.wait_ge(s_mt, 1 if first else h + 1)
                            nc.vector.tensor_copy(max_full, ps[0:NT, 0, 0:P]).then_inc(s_mc, 1)
                            dve.wait_ge(s_mc, 1 if first else h + 1)
                            if not first:
                                dve.wait_ge(s_md, h * 16 * SHIFT)
                            nc.vector.tensor_copy(max_parts[0], max_full).then_inc(s_m1, 1)
                            dve.wait_ge(s_m1, 1 if first else h + 1)
                            nc.vector.tensor_tensor(max_rest, max_full, max_parts[0], ALU.subtract).then_inc(s_m2, 1)
                            dve.wait_ge(s_m2, 1 if first else h + 1)
                            nc.vector.tensor_copy(max_parts[1], max_rest).then_inc(s_m3, 1)
                            dve.wait_ge(s_m3, 1 if first else h + 1)
                            nc.vector.tensor_tensor(max_parts[2], max_rest, max_parts[1], ALU.subtract
                                                    ).then_inc(s_mo, 1)
                        head(0, True)
                        with dve.Fori(1, H) as h:
                            head(h, False)

            s_qk, s_exp, s_pv, s_u = sem(f"scores{l}"), sem(f"exps{l}"), sem(f"pv{l}"), sem(f"pv_copied{l}")
            s_copy, s_inv = sem(f"pv_saved{l}"), sem(f"sums_inverted{l}")
            s_fill, s_ends = sem(f"list_filled{l}"), sem(f"x_normed{l}")
            s_full7, s_read7 = sem(f"bank7_full{l}"), sem(f"bank7_read{l}")
            s_on, s_oc = sem(f"o_normed{l}"), [sem(f"oT_in{l}_{i}") for i in range(2)]
            s_xup = [sem(f"x_updated{l}_{i}") for i in range(2)]
            NU = 2 + (4 if L.mlp else 0)

            def use(b, k):
                return (b - 1) * NU + k + 1

            with nc.Block() as block:
                @block.tensor
                def _(pe):
                    def scores(b, w):
                        g, c = divmod(w, NC)
                        if c == 0:
                            pe.wait_ge(s_q2[g], (b + 1) * 16 * 7)
                        for half in range(2):
                            u = 2 * w + half
                            buf = 2 * (u % SB)
                            last_read = u - SB if u >= SB else max(v for v in range(STEPS) if v % SB == u % SB) - STEPS
                            if not (isinstance(b, int) and b == 0 and u < SB):
                                pe.wait_ge(s_exp, b * STEPS + last_read + 1)
                            for j in range(2):
                                h = HG * g + 2 * half + j
                                last = nc.tensor.matmul(ps[:, buf + j, :], k2[0:ROWS + SHIFT, h, c * P:(c + 1) * P],
                                                        q2[0:ROWS + SHIFT, h, :], start=True, stop=True)
                            last.then_inc(s_qk, 1)

                    def weigh(b, w):
                        g, c = divmod(w, NC)
                        pe.wait_ge(s_exp, b * STEPS + 2 * w + 2)
                        peeled = isinstance(b, int) and b == 0
                        if c == 0 and not (peeled and g < 2):
                            pe.wait_ge(s_u, b * NG + g - 1)
                            if g == 1:
                                pe.wait_ge(s_read7, b * NU)
                        for j in range(HG):
                            last = nc.tensor.matmul(ps[j * VW:(j + 1) * VW, 6 + g % 2, :], v_aug[:, c, HG * g + j, :],
                                                    probs[:, w % 2, j, :], start=(c == 0), stop=(c == NC - 1),
                                                    skip_group_check=True)
                        last.then_inc(s_pv, 1)

                    def hidden(b, f, n):
                        if f == 0:
                            for i in range(2):
                                pe.wait_ge(s_oc[i], (b + 1) * 16 * HG * NG // 2)
                        pe.wait_ge(s_read7, n - 1)
                        for k in range(KD):
                            last = nc.tensor.matmul(ps[:, 7, :], w1[:, k, f * P:(f + 1) * P], oT[:, k, :],
                                                    start=(k == 0), stop=(k == KD - 1))
                        last.then_inc(s_full7, 1)

                    def output(b, pair, half, n):
                        if half == 0:
                            for i in range(2):
                                pe.wait_ge(s_oc[i], (b + 1) * 16 * HG * NG // 2)
                            pe.wait_ge(s_read7, n - 1)
                        src, ks = (hidT, 4) if L.mlp else (oT, KD)
                        t = 2 * pair + half
                        for k in range(ks):
                            last = nc.tensor.matmul(ps[:, 7, half * D:(half + 1) * D], src[:, k, t * P:(t + 1) * P],
                                                    w2[:, k, :], start=(k == 0), stop=(k == ks - 1),
                                                    skip_group_check=True)
                        if half == 1:
                            last.then_inc(s_full7, 1)

                    def tail(b, w):
                        k = 4 if L.mlp else 0
                        if L.mlp and 5 <= w < 9:
                            hidden(b - 1, w - 5, use(b, w - 5))
                        elif 9 <= w < 13:
                            pair, half = divmod(w - 9, 2)
                            output(b - 1, pair, half, use(b, k + pair))

                    def body(b, first):
                        for w in range(NG * NC):
                            scores(b, w)
                            if w > 0:
                                weigh(b, w - 1)
                            elif not first:
                                weigh(b - 1, NG * NC - 1)
                            if not first:
                                tail(b, w)

                    body(0, True)
                    with pe.Fori(1, NB) as b:
                        body(b, False)
                    weigh(NB - 1, NG * NC - 1)
                    for w in range(NC):
                        tail(NB, w)

                @block.scalar
                def _(act):
                    def body(b, first):
                        for u in range(STEPS):
                            w, half = divmod(u, 2)
                            buf = 2 * (u % SB)
                            act.wait_ge(s_qk, b * STEPS + u + 1)
                            if half == 0 and not (first and w < 2):
                                act.wait_ge(s_pv, b * NG * NC + w - 1)
                            nc.scalar.activation(probs[:, w % 2, 2 * half:2 * half + 2, :], ps[:, buf:buf + 2, :],
                                                 ACT.Exp).then_inc(s_exp, 1)
                    body(0, True)
                    with act.Fori(1, NB) as b:
                        body(b, False)

                @block.vector
                def _(dve):
                    tg = tgate[:, l:l + 1]

                    def group(b, g):
                        n = b * NG + g + 1
                        dve.wait_ge(s_pv, b * NG * NC + NC * (g + 1))
                        nc.vector.tensor_copy(pv_sb, ps[:, 6 + g % 2, :]).then_inc(s_copy, 1)
                        nc.vector.stream_shuffle(out=sums, in_=ps[:, 6 + g % 2, :], mask=[DH] * VW).then_inc(s_u, 1)
                        dve.wait_ge(s_u, n)
                        nc.vector.reciprocal(sums, sums).then_inc(s_inv, 1)
                        dve.wait_ge(s_copy, n)
                        dve.wait_ge(s_inv, n)
                        if g >= 2 or not (isinstance(b, int) and b == 0):
                            dve.wait_ge(s_oc[g % 2], (b * (NG // 2) + g // 2) * 16 * HG)
                        nc.vector.tensor_tensor(o_norm[:, g % 2, :], pv_sb, sums, ALU.mult).then_inc(s_on, 1)
                        dve.drain()

                    def tail(b, now, first_group=None):
                        group(now, NG - 1)
                        k = 0
                        if L.mlp:
                            for f in range(4):
                                dve.wait_ge(s_full7, use(b, k))
                                nc.vector.tensor_scalar(hidT[:, f, :], ps[:, 7, :], b1[:, f:f + 1], 0.0,
                                                        ALU.add, ALU.max).then_inc(s_read7, 1)
                                k += 1
                        for pair in range(2):
                            dve.wait_ge(s_full7, use(b, k))
                            nc.vector.tensor_tensor(y_tmp.rearrange("p (t d) -> p t d", d=D),
                                                    ps[:, 7, :].rearrange("p (t d) -> p t d", d=D), b2[:, :, :],
                                                    ALU.add).then_inc(s_read7, 1)
                            dve.wait_ge(s_read7, use(b, k))
                            rows = x[:, bass.ds(now * TB + 2 * pair, 2), :]
                            nc.vector.scalar_tensor_tensor(out=rows, in0=y_tmp.rearrange("p (t d) -> p t d", d=D),
                                                           scalar=tg, in1=rows, op0=ALU.mult,
                                                           op1=ALU.add).then_inc(s_xup[pair], 1)
                            dve.wait_ge(s_xup[pair], now + 1)
                            k += 1
                        if first_group is not None:
                            group(first_group, 0)

                        def step(_):
                            dve.drain()

                        def tile(tensor):
                            return lambda t: (tensor[:, bass.ds(now * TB + t, 1), :]
                                              .rearrange("p a d -> p (a d)"))

                        norm_rows(step, tile(x), tile(xn)).then_inc(s_ends, 1)

                    def body(b, first):
                        if first:
                            group(b, 0)
                        else:
                            tail(b, b - 1, b)
                        for g in range(1, NG - 1):
                            group(b, g)
                    body(0, True)
                    with dve.Fori(1, NB) as b:
                        body(b, False)
                    tail(NB, NB - 1)
                    dve.wait_ge(s_ends, NB)

                @block.sync
                def _(sp):
                    def gather_heads(b, g):
                        later = g == 0 and not (isinstance(b, int) and b == 0)
                        sp.wait_ge(s_on, b * NG + g + 1)
                        if later:
                            sp.wait_ge(s_xup[1], b)
                        for j in range(HG):
                            h = HG * g + j
                            sp.dma_start(oT[(h % 8) * DH:(h % 8 + 1) * DH, h // 8, :],
                                         o_norm[j * VW:j * VW + DH, g % 2, :]).then_inc(s_oc[g % 2], 16)

                    def body(b, first):
                        if not first:
                            gather_heads(b - 1, NG - 1)
                        at = QB if first else sp.snap((b + 1) % NB * QB)
                        for g in range(NG):
                            sp.wait_ge(s_qk, b * STEPS + 2 * NC * (g + 1))
                            load_q2(sp, at, g)
                            if g < NG - 1:
                                gather_heads(b, g)
                    n = L.tiles + 1 - L.shared
                    sp.dma_start(list_x[l].rearrange("(t p) d -> p t d", p=P)[:, L.shared:, :],
                                 zero[:, :].unsqueeze(1).broadcast_to([P, n, D])).then_inc(s_fill, 16)
                    body(0, True)
                    with sp.Fori(1, NB) as b:
                        body(b, False)
                    gather_heads(NB - 1, NG - 1)
                    sp.wait_ge(s_fill, 16)
                    for g in range(NG):
                        sp.wait_ge(s_q2[g], (NB + 1) * 16 * 7)

        def moe(L):
            l = L.n
            NTL, T = L.tiles, L.slots
            s_w, s_e = sem(f"router_in{l}"), [sem(f"expert_in{l}_{e}") for e in range(L.experts)]
            s_xn, s_xt, s_xtc = sem(f"moe_xn{l}"), sem(f"moe_xT{l}"), sem(f"moe_xTc{l}")
            s_lg, s_oh, s_cnt, s_slot = sem(f"logits{l}"), sem(f"onehot{l}"), sem(f"counts{l}"), sem(f"slots{l}")
            s_mx, s_ex, s_send, s_sh, s_xs = (sem(f"tops{l}"), sem(f"top_exp{l}"), sem(f"rows_sent{l}"),
                                              sem(f"shared_sent{l}"), sem(f"rows_scaled{l}"))

            def load_expert(eng, e):
                if l == 0:
                    src = (("sg", "su", "sd") if e == E else ("rg", "ru", "rd"))
                    for dst, name in zip((w_gate, w_up, w_down), src):
                        w = a[name] if e == E else a[name][e]
                        eng.dma_start(dst[:, e, :, :], w.rearrange("(k p) n -> p k n", p=P)).then_inc(s_e[e], 16)
                else:
                    eng.dma_start(w_gate[:, e, :, :], a["ew1"][e].rearrange("(k p) n -> p k n", p=P)).then_inc(s_e[e], 16)
                    eng.dma_start(w_down[:, e, :, :], a["ew2"][e].rearrange("(k p) n -> p k n", p=P)).then_inc(s_e[e], 16)
                    eng.dma_start(eb1[:, e, :], spread(a["eb1"][e], F)).then_inc(s_e[e], 16)
                    eng.dma_start(eb2[:, e, :], spread(a["eb2"][e], D)).then_inc(s_e[e], 16)

            rxT = [view(work, i * KD * QB, [KD, QB])[0] for i in range(2)]

            with nc.Block() as block:
                @block.sync
                def _(sp):
                    sp.dma_start(rw[:, :, :], a[f"rw{l}"].rearrange("(k p) n -> p k n", p=P)).then_inc(s_w, 16)
                    if l == 1:
                        sp.dma_start(rb[:, :], spread(a["rb1"], E)).then_inc(s_w, 16)
                        sp.dma_start(gamma[:, :], spread(a["gamma"], D)).then_inc(s_w, 16)
                        sp.dma_start(beta[:, :], spread(a["beta"], D)).then_inc(s_w, 16)
                    for e in ([E] if l == 0 else []) + list(range(E)):
                        load_expert(sp, e)
                    if l == 0:
                        sp.dma_start(list_x[0][0:S, :].rearrange("(t p) d -> p t d", p=P), xn[:, :, :]
                                     ).then_inc(s_sh, 16)
                    for q in s_e:
                        sp.wait_ge(q, 16 * (3 if l == 0 else 4))

                @block.tensor
                def _(pe):
                    pe.wait_ge(s_w, 16 if l == 0 else 64)

                    def logits(b):
                        pe.wait_ge(s_xtc, b + 1)
                        for t in range(TB):
                            n = b * TB + t
                            for k in range(KD):
                                last = nc.tensor.matmul(ps[:, 4, n * E:(n + 1) * E],
                                                        rxT[b % 2][:, k, t * P:(t + 1) * P], rw[:, k, :],
                                                        start=(k == 0), stop=(k == KD - 1), skip_group_check=True)
                        if b == NB - 1:
                            last.then_inc(s_lg, 1)

                    for b in range(NB):
                        if b >= 2:
                            pe.wait_ge(s_xtc, b - 1)
                        for t in range(TB):
                            for k in range(KD):
                                last = nc.tensor.transpose(ps[:, 2 * (b % 2) + k, t * P:(t + 1) * P],
                                                           xn[:, b * TB + t, k * P:(k + 1) * P], ident[:, :])
                        last.then_inc(s_xt, 1)
                        if b:
                            logits(b - 1)
                    logits(NB - 1)
                    pe.wait_ge(s_oh, 1)
                    nc.tensor.matmul(ps[:, 5, 0:T * E], below[:, :], oh[:, 0:T, :], start=True, stop=True)
                    nc.tensor.matmul(ps[:, 6, 0:T * E], ones[:, :], oh[:, 0:T, :], start=True, stop=True
                                     ).then_inc(s_cnt, 1)

                @block.scalar
                def _(act):
                    for b in range(NB):
                        act.wait_ge(s_xt, b + 1)
                        nc.scalar.activation(rxT[b % 2], ps[:, 2 * (b % 2):2 * (b % 2) + 2, :],
                                             ACT.Copy).then_inc(s_xtc, 1)
                    act.wait_ge(s_mx, 1)
                    if l == 0:
                        nc.scalar.activation(wts[:, 0, :], mx[:, :, 0], ACT.Exp, scale=-1.0).then_inc(s_ex, 1)
                    else:
                        nc.scalar.activation(wts[:, 0, :], wts[:, 2, :], ACT.Exp).then_inc(s_ex, 1)

                @block.vector
                def _(dve):
                    chain = Chain(dve, f"route_chain{l}")
                    dve.wait_ge(s_lg, 1)
                    logit_ps = ps[:, 4, 0:NT * E].rearrange("p (t e) -> p t e", e=E)
                    if l == 0:
                        chain(nc.vector.tensor_copy(lg[:, :, :], logit_ps))
                    else:
                        chain(nc.vector.tensor_tensor(lg[:, :, :], logit_ps,
                                                      rb[:, :].unsqueeze(1).broadcast_to([P, NT, E]), ALU.add))
                    for t in range(NT):
                        last = nc.vector.max(mx[:, t, :], lg[:, t, :])
                    chain(last)
                    for t in range(NT):
                        last = nc.vector.max_index(ix[:, t, :], mx[:, t, :], lg[:, t, :])
                    chain(last)
                    if l == 1:
                        chain(nc.vector.tensor_tensor(wts[:, 2, :], mx[:, :, 1], mx[:, :, 0], ALU.subtract))
                    chain(nc.vector.tensor_copy(ixf[:, :, :], ix[:, :, :]))
                    for i in range(T):
                        last = nc.vector.tensor_scalar(oh[:, i, :], iota8[:, :], ixf[:, i % NT, i // NT:i // NT + 1],
                                                       None, ALU.is_equal)
                        if i == 0:
                            last.then_inc(s_mx, 1)
                    last.then_inc(s_oh, 1)
                    dve.wait_ge(s_ex, 1)
                    chain(nc.vector.tensor_scalar(wts[:, 1, :], wts[:, 0, :], 1.0, None, ALU.add))
                    chain(nc.vector.reciprocal(wts[:, 2, :], wts[:, 1, :]))
                    if l == 1:
                        chain(nc.vector.tensor_tensor(wts[:, 1, :], wts[:, 0, :], wts[:, 2, :], ALU.mult))
                    else:
                        dve.wait_ge(s_sh, 16)
                        for t in range(NT):
                            last = nc.vector.tensor_scalar(xn[:, t, :], xn[:, t, :], wts[:, 2, t:t + 1], None, ALU.mult)
                        last.then_inc(s_xs, 1)
                    dve.wait_ge(s_cnt, 1)
                    before = ps[:, 5, 0:T * E].rearrange("p (t e) -> p t e", e=E)
                    tots = ps[:, 6, 0:T * E].rearrange("p (t e) -> p t e", e=E)
                    chain(nc.vector.tensor_copy(tot[:, 0:T, :], tots))
                    chain(nc.vector.tensor_copy(scan[0][:, 0:T, :], tots))
                    i, step = 0, 1
                    while step < T:
                        nc.vector.tensor_copy(scan[1 - i][:, 0:step, :], scan[i][:, 0:step, :])
                        chain(nc.vector.tensor_tensor(scan[1 - i][:, step:T, :], scan[i][:, step:T, :],
                                                      scan[i][:, 0:T - step, :], ALU.add))
                        i, step = 1 - i, 2 * step
                    incl, other = scan[i], scan[1 - i]
                    chain(nc.vector.tensor_scalar(padi[:, 0, :], incl[:, T - 1, :], float(P - 1), None, ALU.add))
                    chain(nc.vector.tensor_scalar(padi[:, 1, :], padi[:, 0, :], 7, 7, ALU.logical_shift_right,
                                                  ALU.logical_shift_left))
                    chain(nc.vector.tensor_copy(padc[:, 0, :], padi[:, 1, :]))
                    chain(nc.vector.tensor_copy(ends[0][:, :], padc[:, 0, :]))
                    j, step = 0, 1
                    while step < E:
                        nc.vector.tensor_copy(ends[1 - j][:, 0:step], ends[j][:, 0:step])
                        chain(nc.vector.tensor_tensor(ends[1 - j][:, step:E], ends[j][:, step:E],
                                                      ends[j][:, 0:E - step], ALU.add))
                        j, step = 1 - j, 2 * step
                    end = ends[j]
                    chain(nc.vector.tensor_tensor(padc[:, 1, :], end[:, :], padc[:, 0, :], ALU.subtract))
                    chain(nc.vector.tensor_tensor(other[:, 0:T, :], incl[:, 0:T, :], tot[:, 0:T, :], ALU.subtract))
                    chain(nc.vector.tensor_tensor(incl[:, 0:T, :], before, other[:, 0:T, :], ALU.add))
                    chain(nc.vector.tensor_tensor(other[:, 0:T, :], incl[:, 0:T, :],
                                                  padc[:, 1, :].unsqueeze(1).broadcast_to([P, T, E]), ALU.add))
                    chain(nc.vector.tensor_tensor(incl[:, 0:T, :], other[:, 0:T, :], oh[:, 0:T, :], ALU.mult))
                    chain(nc.vector.tensor_reduce(slotf[:, 0:T], incl[:, 0:T, :], AX.X, ALU.add))
                    nc.vector.tensor_scalar(slot[:, 0:T], slotf[:, 0:T], float(L.shared * P), None, ALU.add
                                            ).then_inc(s_slot, 1)
                    routed = NTL - L.shared
                    chain(nc.vector.memset(tilef[:, :], float(E)))
                    tv = tilef[:, L.shared:NTL]
                    chain(nc.vector.memset(tv, 0.0))
                    for e in range(E - 1):
                        chain(nc.vector.scalar_tensor_tensor(out=tv, in0=iota_tile[:, 0:routed], scalar=end[:, e:e + 1],
                                                             in1=tv, op0=ALU.is_ge, op1=ALU.add))
                    chain(nc.vector.tensor_copy(tile_e[:, :], tilef[:, :]))

                @block.gpsimd
                def _(pool):
                    pool.wait_ge(s_slot, 1)
                    if l == 0:
                        pool.wait_ge(s_xs, 1)
                    for i in range(T):
                        nc.gpsimd.indirect_dma_start(
                            out=list_x[l], out_offset=bass.IndirectOffsetOnAxis(ap=slot[:, i:i + 1], axis=0),
                            in_=xn[:, i % NT, :], in_offset=None).then_inc(s_send, 16)
                    pool.wait_ge(s_send, 16 * T)

            s_ld = [sem(f"rows_in{l}_{i}") for i in range(2)]
            s_st = [sem(f"rows_out{l}_{i}") for i in range(2)]
            s_t, s_tc, s_gu, s_ga, s_h = (sem(f"tile_T{l}"), sem(f"tile_Tc{l}"), sem(f"tile_gu{l}"),
                                          sem(f"tile_act{l}"), sem(f"tile_h{l}"))
            s_ht, s_hc, s_dn, s_y = sem(f"tile_hT{l}"), sem(f"tile_hTc{l}"), sem(f"tile_down{l}"), sem(f"tile_y{l}")
            s_first = sem(f"tile_b1{l}")

            with nc.Block() as block:
                @block.sync
                def _(sp):
                    def load(i, par, first=False):
                        at = i * P if first else sp.snap(i * P)
                        if not first:
                            sp.wait_ge(s_t, i - 1)
                        sp.dma_start(rows_in[par], list_x[l][bass.ds(at, P), :]).then_inc(s_ld[par], 16)

                    def store(i, par):
                        at = i * P if isinstance(i, int) else sp.snap(i * P)
                        sp.wait_ge(s_y, i + 1)
                        sp.dma_start(list_y[l][bass.ds(at, P), :], rows_out[par]).then_inc(s_st[par], 16)

                    load(0, 0, True)
                    load(1, 1, True)
                    with sp.Fori(0, NTL // 2) as pair:
                        for par in range(2):
                            load(pair * 2 + par + 2, par)
                            store(pair * 2 + par, par)
                    store(NTL - 1, 0)
                    sp.wait_ge(s_st[0], 16 * (NTL // 2 + 1))
                    sp.wait_ge(s_st[1], 16 * (NTL // 2))
                    for i in range(2):
                        sp.wait_ge(s_ld[i], 16 * (NTL // 2 + 1))

                @block.tensor
                def _(pe):
                    def expert(i):
                        return pe.value_load(tile_e[0:1, bass.ds(i, 1)], min_val=0, max_val=L.experts - 1)

                    def turn_rows(i, par, half):
                        pe.wait_ge(s_ld[par], 16 * (half + 1))
                        for k in range(KD):
                            last = nc.tensor.transpose(ps[:, par, k * P:(k + 1) * P],
                                                       rows_in[par][:, k * P:(k + 1) * P], ident[:, :])
                        last.then_inc(s_t, 1)

                    def up(i, par):
                        e = expert(i)
                        pe.wait_ge(s_tc, i + 1)
                        for n, w in enumerate([w_gate, w_up] if l == 0 else [w_gate]):
                            for k in range(KD):
                                last = nc.tensor.matmul(ps[:, 2 + 2 * par + n, :], rowsT[par][:, k, :],
                                                        w[:, bass.ds(e, 1), k, :].rearrange("p a n -> p (a n)"),
                                                        start=(k == 0), stop=(k == KD - 1))
                        last.then_inc(s_gu, 1)

                    def turn_hidden(i, par):
                        pe.wait_ge(s_h, i + 1)
                        for k in range(4):
                            last = nc.tensor.transpose(ps[:, 6, k * P:(k + 1) * P], hid[par][:, k * P:(k + 1) * P],
                                                       ident[:, :])
                        last.then_inc(s_ht, 1)

                    def down(i, par, first=False):
                        e = expert(i)
                        pe.wait_ge(s_hc, i + 1)
                        if not first:
                            pe.wait_ge(s_y, i)
                        for k in range(4):
                            last = nc.tensor.matmul(ps[:, 7, 0:D], hT[par][:, k, :],
                                                    w_down[:, bass.ds(e, 1), k, :].rearrange("p a n -> p (a n)"),
                                                    start=(k == 0), stop=(k == 3))
                        last.then_inc(s_dn, 1)

                    def step(i, par, half, first=False):
                        turn_rows(i + 1, 1 - par, half + par)
                        turn_hidden(i, par)
                        up(i + 1, 1 - par)
                        down(i, par, first)

                    turn_rows(0, 0, 0)
                    up(0, 0)
                    step(0, 0, 0, True)
                    step(1, 1, 0)
                    with pe.Fori(1, NTL // 2) as pair:
                        step(pair * 2, 0, pair)
                        step(pair * 2 + 1, 1, pair)
                    turn_hidden(NTL - 1, 0)
                    down(NTL - 1, 0)

                @block.scalar
                def _(act):
                    def first_act(i, par):
                        if l == 0:
                            act.wait_ge(s_gu, i + 1)
                            nc.scalar.activation(act_g[par], ps[:, 2 + 2 * par, :], ACT.Silu).then_inc(s_ga, 1)
                        else:
                            act.wait_ge(s_first, i + 1)
                            nc.scalar.activation(hid[par], act_g[par], ACT.Relu).then_inc(s_h, 1)

                    def copy_hT(i, par):
                        act.wait_ge(s_ht, i + 1)
                        nc.scalar.activation(hT[par], ps[:, 6, :].rearrange("p (k n) -> p k n", n=P),
                                             ACT.Copy).then_inc(s_hc, 1)

                    first_act(0, 0)
                    with act.Fori(0, NTL // 2) as pair:
                        for par in range(2):
                            copy_hT(pair * 2 + par, par)
                            first_act(pair * 2 + par + 1, 1 - par)
                    copy_hT(NTL - 1, 0)

                @block.vector
                def _(dve):
                    def copy_rows(i, par):
                        dve.wait_ge(s_t, i + 1)
                        nc.vector.tensor_copy(rowsT[par], ps[:, par, 0:D].rearrange("p (k n) -> p k n", n=P)
                                              ).then_inc(s_tc, 1)

                    def hidden(i, par):
                        if l == 0:
                            dve.wait_ge(s_ga, i + 1)
                            nc.vector.tensor_tensor(hid[par], act_g[par], ps[:, 3 + 2 * par, :], ALU.mult
                                                    ).then_inc(s_h, 1)
                        else:
                            e = dve.value_load(tile_e[0:1, bass.ds(i, 1)], min_val=0, max_val=E - 1)
                            dve.wait_ge(s_gu, i + 1)
                            nc.vector.tensor_tensor(act_g[par], ps[:, 2 + 2 * par, :],
                                                    eb1[:, bass.ds(e, 1), :].rearrange("p a n -> p (a n)"), ALU.add
                                                    ).then_inc(s_first, 1)

                    def finish(i, par, half, first=False):
                        if l == 1:
                            e = dve.value_load(tile_e[0:1, bass.ds(i, 1)], min_val=0, max_val=E - 1)
                        dve.wait_ge(s_dn, i + 1)
                        if not first:
                            dve.wait_ge(s_st[par], 16 * half)
                        if l == 0:
                            nc.vector.tensor_copy(rows_out[par], ps[:, 7, 0:D]).then_inc(s_y, 1)
                        else:
                            nc.vector.tensor_tensor(rows_out[par], ps[:, 7, 0:D],
                                                    eb2[:, bass.ds(e, 1), :].rearrange("p a n -> p (a n)"), ALU.add
                                                    ).then_inc(s_y, 1)

                    copy_rows(0, 0)
                    hidden(0, 0)
                    copy_rows(1, 1)
                    hidden(1, 1)
                    finish(0, 0, 0, True)
                    copy_rows(2, 0)
                    hidden(2, 0)
                    finish(1, 1, 0, True)
                    copy_rows(3, 1)
                    with dve.Fori(1, NTL // 2 - 1) as pair:
                        hidden(pair * 2 + 1, 1)
                        finish(pair * 2, 0, pair)
                        copy_rows(pair * 2 + 2, 0)
                        hidden(pair * 2 + 2, 0)
                        finish(pair * 2 + 1, 1, pair)
                        copy_rows(pair * 2 + 3, 1)
                    n = NTL // 2 - 1
                    hidden(2 * n + 1, 1)
                    finish(2 * n, 0, n)
                    copy_rows(2 * n + 2, 0)
                    hidden(2 * n + 2, 0)
                    finish(2 * n + 1, 1, n)
                    finish(2 * n + 2, 0, n + 1)

            s_back = [sem(f"rows_back{l}_{t}") for t in range(4)]
            s_ysh = [sem(f"shared_back{l}_{b}") for b in range(NB)]
            s_o, s_xf = sem(f"out{l}"), sem(f"x_final{l}")
            with nc.Block() as block:
                @block.gpsimd
                def _(pool):
                    for t in range(NT):
                        for k in range(L.top):
                            i = k * NT + t
                            nc.gpsimd.indirect_dma_start(
                                out=got[k][:, t, :], out_offset=None, in_=list_y[l],
                                in_offset=bass.IndirectOffsetOnAxis(ap=slot[:, i:i + 1], axis=0)
                            ).then_inc(s_back[t // TB], 16)

                @block.sync
                def _(sp):
                    if l == 0:
                        for b in range(NB):
                            sp.dma_start(got[1][:, b * TB:(b + 1) * TB, :],
                                         list_y[0][b * QB:(b + 1) * QB, :].rearrange("(t p) d -> p t d", p=P)
                                         ).then_inc(s_ysh[b], 16)
                    else:
                        dst = out.rearrange("o (t p) d -> p (o t) d", p=P)
                        for b in range(NB):
                            sp.wait_ge(s_xf, b + 1)
                            sp.dma_start(dst[:, b * TB:(b + 1) * TB, :], x[:, b * TB:(b + 1) * TB, :]).then_inc(s_o, 16)
                        sp.wait_ge(s_o, 16 * NB)

                @block.vector
                def _(dve):
                    tg = tgate[:, 2 + l:3 + l]
                    chain = Chain(dve, f"back_chain{l}")
                    if l == 1:
                        nc.vector.tensor_scalar(gamma[:, :], gamma[:, :], tg, None, ALU.mult)
                        chain(nc.vector.tensor_scalar(beta[:, :], beta[:, :], tg, None, ALU.mult))
                    for b in range(NB):
                        ts = slice(b * TB, (b + 1) * TB)
                        dve.wait_ge(s_back[b], 16 * TB * L.top)
                        if l == 0:
                            dve.wait_ge(s_ysh[b], 16)
                            chain(nc.vector.tensor_tensor(got[0][:, ts, :], got[0][:, ts, :], got[1][:, ts, :], ALU.add))
                            chain(nc.vector.scalar_tensor_tensor(
                                out=x[:, ts, :].rearrange("p t d -> p (t d)"),
                                in0=got[0][:, ts, :].rearrange("p t d -> p (t d)"), scalar=tg,
                                in1=x[:, ts, :].rearrange("p t d -> p (t d)"), op0=ALU.mult, op1=ALU.add))
                            continue
                        for t in range(b * TB, (b + 1) * TB):
                            last = nc.vector.scalar_tensor_tensor(out=xn[:, t, :], in0=got[0][:, t, :],
                                                                  scalar=wts[:, 2, t:t + 1], in1=xn[:, t, :],
                                                                  op0=ALU.mult, op1=ALU.add)
                        chain(last)
                        for t in range(b * TB, (b + 1) * TB):
                            last = nc.vector.scalar_tensor_tensor(out=got[0][:, t, :], in0=got[1][:, t, :],
                                                                  scalar=wts[:, 1, t:t + 1], in1=xn[:, t, :],
                                                                  op0=ALU.mult, op1=ALU.add)
                        chain(last)
                        chain(norm_rows(chain, lambda t: got[0][:, b * TB + t, :], lambda t: got[0][:, b * TB + t, :]))
                        gb = gamma[:, :].unsqueeze(1).broadcast_to([P, TB, D])
                        bb = beta[:, :].unsqueeze(1).broadcast_to([P, TB, D])
                        chain(nc.vector.tensor_tensor(got[0][:, ts, :], got[0][:, ts, :], gb, ALU.mult))
                        chain(nc.vector.tensor_tensor(x[:, ts, :], x[:, ts, :], bb, ALU.add))
                        nc.vector.tensor_tensor(x[:, ts, :], x[:, ts, :], got[0][:, ts, :], ALU.add).then_inc(s_xf, 1)

        def dump():
            s_o = sem("dump")
            with nc.Block() as block:
                @block.sync
                def _(sp):
                    sp.dma_start(out.rearrange("o (t p) d -> p (o t) d", p=P), x[:, :, :]).then_inc(s_o, 16)
                    sp.wait_ge(s_o, 16)

        n = 0
        for L in layers:
            attention(L)
            free_semaphores()
            n += 1
            if n == stage:
                return dump()
            moe(L)
            free_semaphores()
            n += 1
            if n == stage and n < 4:
                return dump()


def layout(inputs, np):
    t = {k: np.asarray(v) for k, v in inputs.items()}
    kv = t["L0_xattn_Wkv"].reshape(H, 2, DH, C)
    bkv = t["L0_xattn_bkv"].reshape(H, 2, DH)
    swap = lambda w: np.ascontiguousarray(np.swapaxes(w, -1, -2))
    flat = np.ascontiguousarray
    col = lambda b: flat(b.reshape(-1, P).T)
    return {
        "x": flat(t["x"]), "ctxT": swap(t["ctx_768"][0]), "g_xattn": t["g_xattn"], "g_ffn": t["g_ffn"],
        "wq0": swap(t["L0_xattn_Wq"]), "bq0": col(t["L0_xattn_bq"]),
        "wk0": swap(kv[:, 0].reshape(D, C)), "wv0": swap(kv[:, 1].reshape(D, C)),
        "bk0": col(flat(bkv[:, 0])), "bv0": flat(bkv[:, 1]).reshape(D),
        "wo": swap(t["L0_xattn_Wo"]), "bo0": t["L0_xattn_bo"],
        "rw0": swap(t["L0_ffn_gate_w"]),
        "sg": swap(t["L0_ffn_shared_gate"]), "su": swap(t["L0_ffn_shared_up"]), "sd": swap(t["L0_ffn_shared_down"]),
        "rg": swap(t["L0_ffn_r_gate"]), "ru": swap(t["L0_ffn_r_up"]), "rd": swap(t["L0_ffn_r_down"]),
        "wq1": t["L1_xattn_Wq"], "bq1": col(t["L1_xattn_bq"]), "wk1": t["L1_xattn_Wk"], "bk1": col(t["L1_xattn_bk"]),
        "wv1": t["L1_xattn_Wv"], "bv1": t["L1_xattn_bv"], "w1": t["L1_xattn_W1"], "b1": col(t["L1_xattn_b1"]),
        "w2": t["L1_xattn_W2"], "bo1": t["L1_xattn_b2"],
        "rw1": t["L1_ffn_Wg"], "rb1": t["L1_ffn_bg"], "ew1": t["L1_ffn_W1"], "eb1": t["L1_ffn_b1"],
        "ew2": t["L1_ffn_W2"], "eb2": t["L1_ffn_b2"], "gamma": t["L1_ffn_gamma"], "beta": t["L1_ffn_beta"],
    }


def kernel(**inputs):
    import numpy as np
    import concourse.bacc as bacc
    from concourse.bass_utils import run_bass_kernel_spmd

    nc = bacc.Bacc("TRN2", target_bir_lowering=False, num_devices=1)
    arrays = {f"in_{k}": v for k, v in layout(inputs, np).items()}
    aps = {k[3:]: nc.dram_tensor(k, v.shape, mybir.dt.from_np(v.dtype), kind="ExternalInput").ap()
           for k, v in arrays.items()}
    out = nc.dram_tensor("out_x", (1, S, D), F32, kind="ExternalOutput").ap()
    build(nc, aps, out)
    r = run_bass_kernel_spmd(nc, [arrays], core_ids=[0])
    return r.results[0]["out_x"]
```
